# Optimizing a Trainium2 kernel written in Bass

```python
import numpy as np
import jax
import jax.numpy as jnp

def _softmax(x, axis=-1):
    return jax.nn.softmax(x, axis=axis)
def _gelu(x):
    return jax.nn.gelu(x, approximate=True)
def _silu(x):
    return jax.nn.silu(x)
def _sigmoid(x):
    return jax.nn.sigmoid(x)
def _layernorm(x, axis=-1, eps=1e-5):
    m = jnp.mean(x, axis=axis, keepdims=True)
    v = jnp.var(x, axis=axis, keepdims=True)
    return (x - m) / jnp.sqrt(v + eps)
def _scatter_add(tgt, idx, src, axis=0):
    return tgt.at[idx].add(src)
def _segment_sum(src, seg, n):
    return jax.ops.segment_sum(src, seg, n)

kernel_name = 'mk_conv_preact_d4_conv_nhwc192_04aabc'

def setup_inputs(seed: int = 0):
    np.random.seed(seed)
    _w = jnp.asarray
    def _rec_inputs():
        import jax
        import jax.numpy as jnp
        _gk = jax.random.key(seed)
        x = -9.309e-05 + 1 * jax.random.normal(jax.random.fold_in(_gk, 1), (8, 56, 56, 192), jnp.float32)
        return x
    x = _rec_inputs()
    def _L0_conv_setup():
        import jax, jax.numpy as jnp
        import numpy as np
        HEADS = 6
        K = 3
        PAD = 1

        def _outlook(x, Wv, Wa, ba, Wp, bp):
            B, H, W, C = x.shape
            hd = C // HEADS
            scale = hd ** (-0.5)
            k2 = K * K
            hw = H * W
            v = jnp.einsum('bhwc,cd->bdhw', x, Wv)
            vp = jnp.pad(v, ((0, 0), (0, 0), (PAD, PAD), (PAD, PAD)))
            patches = jnp.stack([vp[:, :, i:i + H, j:j + W] for i in range(K) for j in range(K)], axis=2)
            v = patches.reshape(B, HEADS, hd, k2, hw).transpose(0, 1, 4, 3, 2)
            a = x.reshape(B, hw, C) @ Wa + ba
            a = a.reshape(B, hw, HEADS, k2, k2).transpose(0, 2, 1, 3, 4)
            a = jax.nn.softmax(a * scale, axis=-1)
            out = jnp.einsum('bnpkq,bnpqd->bnpkd', a, v)
            cols = out.transpose(0, 1, 4, 3, 2).reshape(B, C, K, K, H, W)
            acc = jnp.zeros((B, C, H + 2 * PAD, W + 2 * PAD), x.dtype)
            for i in range(K):
                for j in range(K):
                    acc = acc.at[:, :, i:i + H, j:j + W].add(cols[:, :, i, j])
            y = acc[:, :, PAD:PAD + H, PAD:PAD + W].transpose(0, 2, 3, 1)
            return y @ Wp + bp
        key = jax.random.key(seed)
        ks = jax.random.split(key, 6)
        B, H, W, C = (8, 56, 56, 192)
        k4h = K ** 4 * HEADS
        s = 0.02
        return {'x': jax.random.normal(ks[0], (B, H, W, C), jnp.float32), 'Wv': jax.random.normal(ks[1], (C, C), jnp.float32) * s, 'Wa': jax.random.normal(ks[2], (C, k4h), jnp.float32) * s, 'ba': jnp.zeros((k4h,), jnp.float32), 'Wp': jax.random.normal(ks[3], (C, C), jnp.float32) * s, 'bp': jnp.zeros((C,), jnp.float32)}
    _L0_conv_all = _L0_conv_setup()
    _L0_conv_in = {k: v for k, v in _L0_conv_all.items() if k in ('Wv', 'Wa', 'ba', 'Wp', 'bp', )}
    del _L0_conv_all

    def _L1_conv_setup():
        import math
        import jax, jax.numpy as jnp
        import numpy as np
        C_DIM, N_STATE, K_DIR = (192, 16, 4)
        D_RANK = math.ceil(C_DIM / 16)
        B_SZ, H_SZ, W_SZ = (2, 64, 64)

        def _ss2d(x, in_proj_w, conv_w, conv_b, x_proj_w, dt_w, dt_b, A_logs, Ds, ln_g, ln_b, out_w):
            B, H, W, C = x.shape
            L = H * W
            dr = dt_w.shape[1]
            N = A_logs.shape[-1]
            K = A_logs.shape[0]
            xz = x @ in_proj_w
            x_ssm, z = (xz[..., :C], xz[..., C:])
            xc = jnp.transpose(x_ssm, (0, 3, 1, 2))
            xc = jax.lax.conv_general_dilated(xc, conv_w, (1, 1), 'SAME', feature_group_count=C)
            xc = jax.nn.silu(xc + conv_b[None, :, None, None])
            x0 = xc.reshape(B, C, L)
            x1 = x0[..., ::-1]
            x2 = jnp.transpose(xc, (0, 1, 3, 2)).reshape(B, C, L)
            x3 = x2[..., ::-1]
            xs = jnp.stack([x0, x1, x2, x3], axis=0)
            proj = jnp.einsum('kbcl,kcd->kbld', xs, x_proj_w)
            dpart = proj[..., :dr]
            Bm = proj[..., dr:dr + N]
            Cm = proj[..., dr + N:]
            delta = jnp.einsum('kblr,krc->kblc', dpart, dt_w) + dt_b[:, None, None, :]
            delta = jax.nn.softplus(delta + dt_b[:, None, None, :])
            A_neg = -jnp.exp(A_logs)
            u_t = jnp.transpose(xs, (3, 0, 1, 2))
            d_t = jnp.transpose(delta, (2, 0, 1, 3))
            B_t = jnp.transpose(Bm, (2, 0, 1, 3))
            C_t = jnp.transpose(Cm, (2, 0, 1, 3))

            def step(state, inp):
                d, b, c, uu = inp
                dA = jnp.exp(d[..., None] * A_neg[:, None, :, :])
                state = dA * state + (d * uu)[..., None] * b[:, :, None, :]
                y = jnp.einsum('kbcn,kbn->kbc', state, c)
                return (state, y)
            init = jnp.zeros((K, B, C, N), jnp.float32)
            _, ys = jax.lax.scan(step, init, (d_t, B_t, C_t, u_t))
            ys = jnp.transpose(ys, (1, 2, 3, 0))
            ys = ys + Ds[:, None, :, None] * xs
            y0 = ys[0].reshape(B, C, H, W)
            y1 = ys[1][..., ::-1].reshape(B, C, H, W)
            y2 = jnp.transpose(ys[2].reshape(B, C, W, H), (0, 1, 3, 2))
            y3 = jnp.transpose(ys[3][..., ::-1].reshape(B, C, W, H), (0, 1, 3, 2))
            y = y0 + y1 + y2 + y3
            y = jnp.transpose(y, (0, 2, 3, 1))
            mu = y.mean(-1, keepdims=True)
            var = y.var(-1, keepdims=True)
            y = (y - mu) / jnp.sqrt(var + 1e-05) * ln_g + ln_b
            y = y * jax.nn.silu(z)
            return y @ out_w
        key = jax.random.key(seed)
        ks = jax.random.split(key, 8)
        C, N, K, dr = (C_DIM, N_STATE, K_DIR, D_RANK)
        x = jax.random.normal(ks[0], (B_SZ, H_SZ, W_SZ, C), jnp.float32)
        in_proj_w = jax.random.normal(ks[1], (C, 2 * C), jnp.float32) / math.sqrt(C)
        conv_w = jax.random.normal(ks[2], (C, 1, 3, 3), jnp.float32) * 0.1
        conv_b = jnp.zeros((C,), jnp.float32)
        x_proj_w = jax.random.normal(ks[3], (K, C, dr + 2 * N), jnp.float32) / math.sqrt(C)
        dt_w = jax.random.normal(ks[4], (K, dr, C), jnp.float32) / math.sqrt(dr)
        dt_min, dt_max, floor = (0.001, 0.1, 0.0001)
        r = jax.random.uniform(ks[5], (K, C), jnp.float32)
        dt_init = jnp.clip(jnp.exp(r * (math.log(dt_max) - math.log(dt_min)) + math.log(dt_min)), floor, None)
        dt_b = dt_init + jnp.log(-jnp.expm1(-dt_init))
        A_logs = jnp.tile(jnp.log(jnp.arange(1, N + 1, dtype=jnp.float32))[None, None, :], (K, C, 1))
        Ds = jnp.ones((K, C), jnp.float32)
        ln_g = jnp.ones((C,), jnp.float32)
        ln_b = jnp.zeros((C,), jnp.float32)
        out_w = jax.random.normal(ks[6], (C, C), jnp.float32) / math.sqrt(C)
        return dict(x=x, in_proj_w=in_proj_w, conv_w=conv_w, conv_b=conv_b, x_proj_w=x_proj_w, dt_w=dt_w, dt_b=dt_b, A_logs=A_logs, Ds=Ds, ln_g=ln_g, ln_b=ln_b, out_w=out_w)
    _L1_conv_all = _L1_conv_setup()
    _L1_conv_in = {k: v for k, v in _L1_conv_all.items() if k in ('in_proj_w', 'conv_w', 'conv_b', 'x_proj_w', 'dt_w', 'dt_b', 'A_logs', 'Ds', 'ln_g', 'ln_b', 'out_w', )}
    del _L1_conv_all

    def _L2_conv_setup():
        import jax, jax.numpy as jnp
        import numpy as np
        from jax import lax
        DIM = 192

        def s6_scan(x, A, Bv, Cv, Dv, res_scale):
            N, L, C = x.shape
            h0 = jnp.zeros((N, C), dtype=x.dtype)
            dr = Dv + res_scale

            def step(h, xt):
                h = jnp.matmul(h, A) + Bv * xt
                y = Cv * h + dr * xt
                return (h, y)
            _, ys = lax.scan(step, h0, jnp.swapaxes(x, 0, 1))
            return jnp.swapaxes(ys, 0, 1)
        key = jax.random.key(seed)
        k1, k2, k3, k4, k5 = jax.random.split(key, 5)
        B, H, W, C = (8, 128, 128, DIM)
        x = jax.random.normal(k1, (B, H, W, C), dtype=jnp.float32)
        A = 0.05 * jax.random.normal(k2, (C, C), dtype=jnp.float32)
        Bv = jax.random.normal(k3, (C,), dtype=jnp.float32)
        Cv = jax.random.normal(k4, (C,), dtype=jnp.float32)
        Dv = jax.random.normal(k5, (C,), dtype=jnp.float32)
        res_scale = jnp.ones((1,), dtype=jnp.float32)
        return {'x': x, 'A': A, 'Bv': Bv, 'Cv': Cv, 'Dv': Dv, 'res_scale': res_scale}
    _L2_conv_all = _L2_conv_setup()
    _L2_conv_in = {k: v for k, v in _L2_conv_all.items() if k in ('A', 'Bv', 'Cv', 'Dv', 'res_scale', )}
    del _L2_conv_all

    def _L3_conv_setup():
        import jax, jax.numpy as jnp
        import numpy as np
        import math
        D_MODEL = 192
        SSM_RATIO = 2.0
        D_STATE = 16
        D_CONV = 3
        D_INNER = int(SSM_RATIO * D_MODEL)
        DT_RANK = math.ceil(D_MODEL / 16)
        KG = 4
        BATCH, HH, WW = (4, 64, 64)

        def _ss2d(x, in_proj_w, conv_w, conv_b, x_proj_weight, dt_projs_weight, dt_projs_bias, A_logs, Ds, norm_gamma, norm_beta, out_proj_w):
            B, H, W, _ = x.shape
            DI = conv_w.shape[0]
            N = A_logs.shape[1]
            K = x_proj_weight.shape[0]
            R = dt_projs_weight.shape[2]
            L = H * W
            xz = x @ in_proj_w.T
            xp, z = (xz[..., :DI], xz[..., DI:])
            z = jax.nn.silu(z)
            xc = jnp.transpose(xp, (0, 3, 1, 2))
            xc = jax.lax.conv_general_dilated(xc, conv_w, window_strides=(1, 1), padding='SAME', feature_group_count=DI, dimension_numbers=('NCHW', 'OIHW', 'NCHW'))
            xc = jax.nn.silu(xc + conv_b[None, :, None, None])
            x0 = xc.reshape(B, DI, L)
            x1 = jnp.swapaxes(xc, 2, 3).reshape(B, DI, L)
            xs = jnp.stack([x0, x1, x0[..., ::-1], x1[..., ::-1]], axis=1)
            x_dbl = jnp.einsum('bkdl,kcd->bkcl', xs, x_proj_weight)
            dts_r = x_dbl[:, :, :R]
            Bs = x_dbl[:, :, R:R + N]
            Cs = x_dbl[:, :, R + N:]
            dts = jnp.einsum('bkrl,kdr->bkdl', dts_r, dt_projs_weight)
            A = -jnp.exp(A_logs).reshape(K, DI, N)
            delta = jax.nn.softplus(dts + dt_projs_bias[None, :, :, None])
            u_t = jnp.moveaxis(xs, -1, 0)
            d_t = jnp.moveaxis(delta, -1, 0)
            B_t = jnp.moveaxis(Bs, -1, 0)
            C_t = jnp.moveaxis(Cs, -1, 0)

            def step(h, inp):
                u_l, dt_l, Bl, Cl = inp
                dA = jnp.exp(dt_l[..., None] * A[None])
                h = dA * h + (dt_l * u_l)[..., None] * Bl[:, :, None, :]
                y = jnp.sum(h * Cl[:, :, None, :], axis=-1)
                return (h, y)
            h0 = jnp.zeros((B, K, DI, N), dtype=xs.dtype)
            _, ys = jax.lax.scan(step, h0, (u_t, d_t, B_t, C_t))
            out_y = jnp.moveaxis(ys, 0, -1)
            out_y = out_y + Ds.reshape(K, DI)[None, :, :, None] * xs
            inv_y = out_y[:, 2:4, :, ::-1]
            wh_y = jnp.swapaxes(out_y[:, 1].reshape(B, DI, W, H), 2, 3).reshape(B, DI, L)
            invwh_y = jnp.swapaxes(inv_y[:, 1].reshape(B, DI, W, H), 2, 3).reshape(B, DI, L)
            y = out_y[:, 0] + inv_y[:, 0] + wh_y + invwh_y
            y = jnp.swapaxes(y, 1, 2).reshape(B, H, W, DI)
            mu = jnp.mean(y, axis=-1, keepdims=True)
            var = jnp.var(y, axis=-1, keepdims=True)
            y = (y - mu) / jnp.sqrt(var + 1e-05) * norm_gamma + norm_beta
            y = y * z
            return y @ out_proj_w.T
        key = jax.random.key(seed)
        ks = jax.random.split(key, 10)
        x = jax.random.normal(ks[0], (BATCH, HH, WW, D_MODEL), dtype=jnp.float32)
        in_proj_w = jax.random.normal(ks[1], (2 * D_INNER, D_MODEL), dtype=jnp.float32) * 0.02
        conv_w = jax.random.normal(ks[2], (D_INNER, 1, D_CONV, D_CONV), dtype=jnp.float32) * 0.1
        conv_b = jnp.zeros((D_INNER,), dtype=jnp.float32)
        x_proj_weight = jax.random.normal(ks[3], (KG, DT_RANK + 2 * D_STATE, D_INNER), dtype=jnp.float32) * 0.02
        dt_std = DT_RANK ** (-0.5)
        dt_projs_weight = jax.random.uniform(ks[4], (KG, D_INNER, DT_RANK), dtype=jnp.float32, minval=-dt_std, maxval=dt_std)
        dt = jnp.exp(jax.random.uniform(ks[5], (KG, D_INNER), dtype=jnp.float32) * (math.log(0.1) - math.log(0.001)) + math.log(0.001))
        dt = jnp.clip(dt, 0.0001, None)
        dt_projs_bias = dt + jnp.log(-jnp.expm1(-dt))
        A_logs = jnp.log(jnp.tile(jnp.arange(1, D_STATE + 1, dtype=jnp.float32)[None, :], (KG * D_INNER, 1)))
        Ds = jnp.ones((KG * D_INNER,), dtype=jnp.float32)
        norm_gamma = jnp.ones((D_INNER,), dtype=jnp.float32)
        norm_beta = jnp.zeros((D_INNER,), dtype=jnp.float32)
        out_proj_w = jax.random.normal(ks[6], (D_MODEL, D_INNER), dtype=jnp.float32) * 0.02
        return {'x': x, 'in_proj_w': in_proj_w, 'conv_w': conv_w, 'conv_b': conv_b, 'x_proj_weight': x_proj_weight, 'dt_projs_weight': dt_projs_weight, 'dt_projs_bias': dt_projs_bias, 'A_logs': A_logs, 'Ds': Ds, 'norm_gamma': norm_gamma, 'norm_beta': norm_beta, 'out_proj_w': out_proj_w}
    _L3_conv_all = _L3_conv_setup()
    _L3_conv_in = {k: v for k, v in _L3_conv_all.items() if k in ('in_proj_w', 'conv_w', 'conv_b', 'x_proj_weight', 'dt_projs_weight', 'dt_projs_bias', 'A_logs', 'Ds', 'norm_gamma', 'norm_beta', 'out_proj_w', )}
    del _L3_conv_all

    return {
        "x": x,
        "L0_conv_Wv": _L0_conv_in["Wv"],
        "L0_conv_Wa": _L0_conv_in["Wa"],
        "L0_conv_ba": _L0_conv_in["ba"],
        "L0_conv_Wp": _L0_conv_in["Wp"],
        "L0_conv_bp": _L0_conv_in["bp"],
        "L1_conv_in_proj_w": _L1_conv_in["in_proj_w"],
        "L1_conv_conv_w": _L1_conv_in["conv_w"],
        "L1_conv_conv_b": _L1_conv_in["conv_b"],
        "L1_conv_x_proj_w": _L1_conv_in["x_proj_w"],
        "L1_conv_dt_w": _L1_conv_in["dt_w"],
        "L1_conv_dt_b": _L1_conv_in["dt_b"],
        "L1_conv_A_logs": _L1_conv_in["A_logs"],
        "L1_conv_Ds": _L1_conv_in["Ds"],
        "L1_conv_ln_g": _L1_conv_in["ln_g"],
        "L1_conv_ln_b": _L1_conv_in["ln_b"],
        "L1_conv_out_w": _L1_conv_in["out_w"],
        "L2_conv_A": _L2_conv_in["A"],
        "L2_conv_Bv": _L2_conv_in["Bv"],
        "L2_conv_Cv": _L2_conv_in["Cv"],
        "L2_conv_Dv": _L2_conv_in["Dv"],
        "L2_conv_res_scale": _L2_conv_in["res_scale"],
        "L3_conv_in_proj_w": _L3_conv_in["in_proj_w"],
        "L3_conv_conv_w": _L3_conv_in["conv_w"],
        "L3_conv_conv_b": _L3_conv_in["conv_b"],
        "L3_conv_x_proj_weight": _L3_conv_in["x_proj_weight"],
        "L3_conv_dt_projs_weight": _L3_conv_in["dt_projs_weight"],
        "L3_conv_dt_projs_bias": _L3_conv_in["dt_projs_bias"],
        "L3_conv_A_logs": _L3_conv_in["A_logs"],
        "L3_conv_Ds": _L3_conv_in["Ds"],
        "L3_conv_norm_gamma": _L3_conv_in["norm_gamma"],
        "L3_conv_norm_beta": _L3_conv_in["norm_beta"],
        "L3_conv_out_proj_w": _L3_conv_in["out_proj_w"],
    }

def reference(x, L0_conv_Wv, L0_conv_Wa, L0_conv_ba, L0_conv_Wp, L0_conv_bp, L1_conv_in_proj_w, L1_conv_conv_w, L1_conv_conv_b, L1_conv_x_proj_w, L1_conv_dt_w, L1_conv_dt_b, L1_conv_A_logs, L1_conv_Ds, L1_conv_ln_g, L1_conv_ln_b, L1_conv_out_w, L2_conv_A, L2_conv_Bv, L2_conv_Cv, L2_conv_Dv, L2_conv_res_scale, L3_conv_in_proj_w, L3_conv_conv_w, L3_conv_conv_b, L3_conv_x_proj_weight, L3_conv_dt_projs_weight, L3_conv_dt_projs_bias, L3_conv_A_logs, L3_conv_Ds, L3_conv_norm_gamma, L3_conv_norm_beta, L3_conv_out_proj_w):
    import jax
    import jax.numpy as jnp
    def _L0_conv_ref(x, Wv, Wa, ba, Wp, bp):
        import jax, jax.numpy as jnp
        import numpy as np
        HEADS = 6
        K = 3
        PAD = 1

        def _outlook(x, Wv, Wa, ba, Wp, bp):
            B, H, W, C = x.shape
            hd = C // HEADS
            scale = hd ** (-0.5)
            k2 = K * K
            hw = H * W
            v = jnp.einsum('bhwc,cd->bdhw', x, Wv)
            vp = jnp.pad(v, ((0, 0), (0, 0), (PAD, PAD), (PAD, PAD)))
            patches = jnp.stack([vp[:, :, i:i + H, j:j + W] for i in range(K) for j in range(K)], axis=2)
            v = patches.reshape(B, HEADS, hd, k2, hw).transpose(0, 1, 4, 3, 2)
            a = x.reshape(B, hw, C) @ Wa + ba
            a = a.reshape(B, hw, HEADS, k2, k2).transpose(0, 2, 1, 3, 4)
            a = jax.nn.softmax(a * scale, axis=-1)
            out = jnp.einsum('bnpkq,bnpqd->bnpkd', a, v)
            cols = out.transpose(0, 1, 4, 3, 2).reshape(B, C, K, K, H, W)
            acc = jnp.zeros((B, C, H + 2 * PAD, W + 2 * PAD), x.dtype)
            for i in range(K):
                for j in range(K):
                    acc = acc.at[:, :, i:i + H, j:j + W].add(cols[:, :, i, j])
            y = acc[:, :, PAD:PAD + H, PAD:PAD + W].transpose(0, 2, 3, 1)
            return y @ Wp + bp
        return _outlook(x, Wv, Wa, ba, Wp, bp)

    def _L1_conv_ref(x, in_proj_w, conv_w, conv_b, x_proj_w, dt_w, dt_b, A_logs, Ds, ln_g, ln_b, out_w):
        import math
        import jax, jax.numpy as jnp
        import numpy as np
        C_DIM, N_STATE, K_DIR = (192, 16, 4)
        D_RANK = math.ceil(C_DIM / 16)
        B_SZ, H_SZ, W_SZ = (2, 64, 64)

        def _ss2d(x, in_proj_w, conv_w, conv_b, x_proj_w, dt_w, dt_b, A_logs, Ds, ln_g, ln_b, out_w):
            B, H, W, C = x.shape
            L = H * W
            dr = dt_w.shape[1]
            N = A_logs.shape[-1]
            K = A_logs.shape[0]
            xz = x @ in_proj_w
            x_ssm, z = (xz[..., :C], xz[..., C:])
            xc = jnp.transpose(x_ssm, (0, 3, 1, 2))
            xc = jax.lax.conv_general_dilated(xc, conv_w, (1, 1), 'SAME', feature_group_count=C)
            xc = jax.nn.silu(xc + conv_b[None, :, None, None])
            x0 = xc.reshape(B, C, L)
            x1 = x0[..., ::-1]
            x2 = jnp.transpose(xc, (0, 1, 3, 2)).reshape(B, C, L)
            x3 = x2[..., ::-1]
            xs = jnp.stack([x0, x1, x2, x3], axis=0)
            proj = jnp.einsum('kbcl,kcd->kbld', xs, x_proj_w)
            dpart = proj[..., :dr]
            Bm = proj[..., dr:dr + N]
            Cm = proj[..., dr + N:]
            delta = jnp.einsum('kblr,krc->kblc', dpart, dt_w) + dt_b[:, None, None, :]
            delta = jax.nn.softplus(delta + dt_b[:, None, None, :])
            A_neg = -jnp.exp(A_logs)
            u_t = jnp.transpose(xs, (3, 0, 1, 2))
            d_t = jnp.transpose(delta, (2, 0, 1, 3))
            B_t = jnp.transpose(Bm, (2, 0, 1, 3))
            C_t = jnp.transpose(Cm, (2, 0, 1, 3))

            def step(state, inp):
                d, b, c, uu = inp
                dA = jnp.exp(d[..., None] * A_neg[:, None, :, :])
                state = dA * state + (d * uu)[..., None] * b[:, :, None, :]
                y = jnp.einsum('kbcn,kbn->kbc', state, c)
                return (state, y)
            init = jnp.zeros((K, B, C, N), jnp.float32)
            _, ys = jax.lax.scan(step, init, (d_t, B_t, C_t, u_t))
            ys = jnp.transpose(ys, (1, 2, 3, 0))
            ys = ys + Ds[:, None, :, None] * xs
            y0 = ys[0].reshape(B, C, H, W)
            y1 = ys[1][..., ::-1].reshape(B, C, H, W)
            y2 = jnp.transpose(ys[2].reshape(B, C, W, H), (0, 1, 3, 2))
            y3 = jnp.transpose(ys[3][..., ::-1].reshape(B, C, W, H), (0, 1, 3, 2))
            y = y0 + y1 + y2 + y3
            y = jnp.transpose(y, (0, 2, 3, 1))
            mu = y.mean(-1, keepdims=True)
            var = y.var(-1, keepdims=True)
            y = (y - mu) / jnp.sqrt(var + 1e-05) * ln_g + ln_b
            y = y * jax.nn.silu(z)
            return y @ out_w
        return _ss2d(x, in_proj_w, conv_w, conv_b, x_proj_w, dt_w, dt_b, A_logs, Ds, ln_g, ln_b, out_w)

    def _L2_conv_ref(x, A, Bv, Cv, Dv, res_scale):
        import jax, jax.numpy as jnp
        import numpy as np
        from jax import lax
        DIM = 192

        def s6_scan(x, A, Bv, Cv, Dv, res_scale):
            N, L, C = x.shape
            h0 = jnp.zeros((N, C), dtype=x.dtype)
            dr = Dv + res_scale

            def step(h, xt):
                h = jnp.matmul(h, A) + Bv * xt
                y = Cv * h + dr * xt
                return (h, y)
            _, ys = lax.scan(step, h0, jnp.swapaxes(x, 0, 1))
            return jnp.swapaxes(ys, 0, 1)
        B, H, W, C = x.shape
        horiz = jnp.transpose(x, (0, 2, 1, 3)).reshape(B * W, H, C)
        y_h = s6_scan(horiz, A, Bv, Cv, Dv, res_scale).reshape(B, W, H, C)
        y_h = jnp.transpose(y_h, (0, 2, 1, 3))
        vert = x.reshape(B * H, W, C)
        y_v = s6_scan(vert, A, Bv, Cv, Dv, res_scale).reshape(B, H, W, C)
        dlen = min(H, W)
        idx = jnp.arange(dlen)
        diag_in = x[:, idx, idx, :]
        anti_in = x[:, idx, W - 1 - idx, :]
        diag_p = s6_scan(diag_in, A, Bv, Cv, Dv, res_scale)
        anti_p = s6_scan(anti_in, A, Bv, Cv, Dv, res_scale)
        zeros = jnp.zeros_like(x)
        diag_map = zeros.at[:, idx, idx, :].set(diag_p)
        anti_map = zeros.at[:, idx, W - 1 - idx, :].set(anti_p)
        return y_h + y_v + diag_map + anti_map

    def _L3_conv_ref(x, in_proj_w, conv_w, conv_b, x_proj_weight, dt_projs_weight, dt_projs_bias, A_logs, Ds, norm_gamma, norm_beta, out_proj_w):
        import jax, jax.numpy as jnp
        import numpy as np
        import math
        D_MODEL = 192
        SSM_RATIO = 2.0
        D_STATE = 16
        D_CONV = 3
        D_INNER = int(SSM_RATIO * D_MODEL)
        DT_RANK = math.ceil(D_MODEL / 16)
        KG = 4
        BATCH, HH, WW = (4, 64, 64)

        def _ss2d(x, in_proj_w, conv_w, conv_b, x_proj_weight, dt_projs_weight, dt_projs_bias, A_logs, Ds, norm_gamma, norm_beta, out_proj_w):
            B, H, W, _ = x.shape
            DI = conv_w.shape[0]
            N = A_logs.shape[1]
            K = x_proj_weight.shape[0]
            R = dt_projs_weight.shape[2]
            L = H * W
            xz = x @ in_proj_w.T
            xp, z = (xz[..., :DI], xz[..., DI:])
            z = jax.nn.silu(z)
            xc = jnp.transpose(xp, (0, 3, 1, 2))
            xc = jax.lax.conv_general_dilated(xc, conv_w, window_strides=(1, 1), padding='SAME', feature_group_count=DI, dimension_numbers=('NCHW', 'OIHW', 'NCHW'))
            xc = jax.nn.silu(xc + conv_b[None, :, None, None])
            x0 = xc.reshape(B, DI, L)
            x1 = jnp.swapaxes(xc, 2, 3).reshape(B, DI, L)
            xs = jnp.stack([x0, x1, x0[..., ::-1], x1[..., ::-1]], axis=1)
            x_dbl = jnp.einsum('bkdl,kcd->bkcl', xs, x_proj_weight)
            dts_r = x_dbl[:, :, :R]
            Bs = x_dbl[:, :, R:R + N]
            Cs = x_dbl[:, :, R + N:]
            dts = jnp.einsum('bkrl,kdr->bkdl', dts_r, dt_projs_weight)
            A = -jnp.exp(A_logs).reshape(K, DI, N)
            delta = jax.nn.softplus(dts + dt_projs_bias[None, :, :, None])
            u_t = jnp.moveaxis(xs, -1, 0)
            d_t = jnp.moveaxis(delta, -1, 0)
            B_t = jnp.moveaxis(Bs, -1, 0)
            C_t = jnp.moveaxis(Cs, -1, 0)

            def step(h, inp):
                u_l, dt_l, Bl, Cl = inp
                dA = jnp.exp(dt_l[..., None] * A[None])
                h = dA * h + (dt_l * u_l)[..., None] * Bl[:, :, None, :]
                y = jnp.sum(h * Cl[:, :, None, :], axis=-1)
                return (h, y)
            h0 = jnp.zeros((B, K, DI, N), dtype=xs.dtype)
            _, ys = jax.lax.scan(step, h0, (u_t, d_t, B_t, C_t))
            out_y = jnp.moveaxis(ys, 0, -1)
            out_y = out_y + Ds.reshape(K, DI)[None, :, :, None] * xs
            inv_y = out_y[:, 2:4, :, ::-1]
            wh_y = jnp.swapaxes(out_y[:, 1].reshape(B, DI, W, H), 2, 3).reshape(B, DI, L)
            invwh_y = jnp.swapaxes(inv_y[:, 1].reshape(B, DI, W, H), 2, 3).reshape(B, DI, L)
            y = out_y[:, 0] + inv_y[:, 0] + wh_y + invwh_y
            y = jnp.swapaxes(y, 1, 2).reshape(B, H, W, DI)
            mu = jnp.mean(y, axis=-1, keepdims=True)
            var = jnp.var(y, axis=-1, keepdims=True)
            y = (y - mu) / jnp.sqrt(var + 1e-05) * norm_gamma + norm_beta
            y = y * z
            return y @ out_proj_w.T
        return _ss2d(x, in_proj_w, conv_w, conv_b, x_proj_weight, dt_projs_weight, dt_projs_bias, A_logs, Ds, norm_gamma, norm_beta, out_proj_w)

    def _gn(v, G=32, eps=1e-5):
        B_, H_, W_, C_ = v.shape
        g = v.reshape(B_, H_, W_, G, C_ // G)
        m = jnp.mean(g, axis=(1, 2, 4), keepdims=True)
        s = jnp.var(g, axis=(1, 2, 4), keepdims=True)
        return ((g - m) / jnp.sqrt(s + eps)).reshape(v.shape)

    def _ln_c(v, eps=1e-6):
        m = jnp.mean(v, axis=-1, keepdims=True)
        s = jnp.var(v, axis=-1, keepdims=True)
        return (v - m) / jnp.sqrt(s + eps)

    def _ln_t(v, eps=1e-5):
        m = jnp.mean(v, axis=-1, keepdims=True)
        s = jnp.var(v, axis=-1, keepdims=True)
        return (v - m) / jnp.sqrt(s + eps)

    def _to_tokens(v):
        B_, H_, W_, C_ = v.shape
        return v.reshape(B_, H_ * W_, C_)
    def _from_tokens(t, like):
        return t.reshape(like.shape)

    x = x + _L0_conv_ref(_gn(x), L0_conv_Wv, L0_conv_Wa, L0_conv_ba, L0_conv_Wp, L0_conv_bp)
    x = x + _L1_conv_ref(_gn(x), L1_conv_in_proj_w, L1_conv_conv_w, L1_conv_conv_b, L1_conv_x_proj_w, L1_conv_dt_w, L1_conv_dt_b, L1_conv_A_logs, L1_conv_Ds, L1_conv_ln_g, L1_conv_ln_b, L1_conv_out_w)
    x = x + _L2_conv_ref(_gn(x), L2_conv_A, L2_conv_Bv, L2_conv_Cv, L2_conv_Dv, L2_conv_res_scale)
    x = x + _L3_conv_ref(_gn(x), L3_conv_in_proj_w, L3_conv_conv_w, L3_conv_conv_b, L3_conv_x_proj_weight, L3_conv_dt_projs_weight, L3_conv_dt_projs_bias, L3_conv_A_logs, L3_conv_Ds, L3_conv_norm_gamma, L3_conv_norm_beta, L3_conv_out_proj_w)
    return x


_drawn_inputs = setup_inputs


def setup_inputs(seed=0):
    import zlib

    import numpy as np

    out = dict(_drawn_inputs(seed))
    spreads = {'L0_conv_ba': (0.0, 0.8),
     'L0_conv_bp': (0.0, 0.1),
     'L1_conv_conv_b': (0.0, 0.1),
     'L1_conv_Ds': (1.0, 0.2),
     'L1_conv_ln_g': (1.0, 0.2),
     'L1_conv_ln_b': (0.0, 0.1),
     'L3_conv_conv_b': (0.0, 0.771),
     'L3_conv_Ds': (1.0, 0.6),
     'L3_conv_norm_gamma': (1.0, 0.6),
     'L3_conv_norm_beta': (0.0, 0.8)}
    factors = {'L0_conv_Wa': 8.0,
     'L1_conv_x_proj_w': 8.0,
     'L1_conv_dt_w': 8.0,
     'L1_conv_dt_b': 8.0,
     'L1_conv_A_logs': 8.0,
     'L3_conv_in_proj_w': 4.466,
     'L3_conv_conv_w': 6.801,
     'L3_conv_x_proj_weight': 8.0,
     'L3_conv_dt_projs_weight': 8.0,
     'L3_conv_dt_projs_bias': 8.0,
     'L3_conv_A_logs': 8.0,
     'L3_conv_out_proj_w': 4.438}
    for name, (base, spread) in spreads.items():
        noise = np.random.default_rng([zlib.crc32(name.encode()), seed]).standard_normal(out[name].shape)
        drawn = base * np.exp(spread * noise) if base else spread * noise
        out[name] = jnp.asarray(drawn.astype(out[name].dtype))
    for name, factor in factors.items():
        out[name] = (out[name] * factor).astype(out[name].dtype)
    return out
```

```python
import math
import concourse.bass as bass
from concourse import mybir
from contextlib import ExitStack

SIDE = 56
PIX = SIDE * SIDE
CHUNK = 7 * SIDE
CHUNKS = PIX // CHUNK
PADDED = (SIDE + 2) * (SIDE + 2)
STATES = 16
RANK = 12
DIRS = {"L1": [(0, False), (0, True), (1, False), (1, True)],
        "L3": [(0, False), (1, False), (0, True), (1, True)]}
SMALL = 1 / 64
ROOT = math.sqrt(1 / 3)
LAYERS = ["L0", "L1", "L2", "L3"]
class Norm:

    def __init__(self, sb, sem):
        f32 = mybir.dt.float32
        self.x = sb("x", [96, 2, PIX], f32)
        self.stats = sb("stats", [96, 2, CHUNKS, 6], f32)
        self.mv = sb("mv", [96, 2, 2], f32)
        self.gmean = sb("gmean", [96, 2], f32)
        self.gdev = sb("gdev", [96, 2], f32)
        self.grstd = sb("grstd", [96, 2], f32)
        self.group = sb("group", [96, 96], f32)
        self.gn_v = sem("gn_v")
        self.gn_t = sem("gn_t")
        self.gn_s = sem("gn_s")


def norm_vector(nc, dve, g, b, xn, x_loaded):
    ALU = mybir.AluOpType
    dve.wait_ge(x_loaded, b * 16 + 16)
    for t in range(2):
        for c in range(CHUNKS):
            last = nc.vector.bn_stats(g.stats[:, t, c, :], g.x[:, t, c * CHUNK:(c + 1) * CHUNK])
    last.then_inc(g.gn_v, 1)
    dve.wait_ge(g.gn_v, b * 8 + 1)
    nc.vector.tensor_copy(g.gdev[:, :], g.stats[:, :, 0, 0])
    for t in range(2):
        last = nc.vector.bn_aggr(g.mv[:, t, :], g.stats[:, t, :, :])
    last.then_inc(g.gn_v, 1)
    dve.wait_ge(g.gn_t, b * 2 + 1)
    nc.vector.tensor_copy(g.gmean[:, :], g.ps[0:96, 0:2]).then_inc(g.gn_v, 1)
    dve.wait_ge(g.gn_v, b * 8 + 3)
    nc.vector.tensor_tensor(g.gdev[:, :], g.mv[:, :, 0], g.gmean[:, :], ALU.subtract).then_inc(g.gn_v, 1)
    dve.wait_ge(g.gn_v, b * 8 + 4)
    nc.vector.tensor_tensor(g.gdev[:, :], g.gdev[:, :], g.gdev[:, :], ALU.mult).then_inc(g.gn_v, 1)
    dve.wait_ge(g.gn_v, b * 8 + 5)
    nc.vector.tensor_tensor(g.gdev[:, :], g.gdev[:, :], g.mv[:, :, 1], ALU.add).then_inc(g.gn_v, 1)
    dve.wait_ge(g.gn_s, b + 1)
    nc.vector.reciprocal(g.grstd[:, :], g.grstd[:, :]).then_inc(g.gn_v, 1)
    dve.wait_ge(g.gn_v, b * 8 + 7)
    for t in range(2):
        last = nc.vector.tensor_scalar(xn[:, t, :], g.x[:, t, :], g.gmean[:, t:t + 1], g.grstd[:, t:t + 1],
                                       ALU.subtract, ALU.mult)
    last.then_inc(g.gn_v, 1)


def norm_tensor(nc, pe, g, b):
    pe.wait_ge(g.gn_v, b * 8 + 2)
    nc.tensor.matmul(g.ps[0:96, 0:2], g.group[:, :], g.mv[:, :, 0], start=True, stop=True).then_inc(g.gn_t, 1)
    pe.wait_ge(g.gn_v, b * 8 + 6)
    nc.tensor.matmul(g.ps[0:96, 8:10], g.group[:, :], g.gdev[:, :], start=True, stop=True).then_inc(g.gn_t, 1)


def norm_scalar(nc, act, g, b, epsilon):
    act.wait_ge(g.gn_t, b * 2 + 2)
    nc.scalar.activation(g.grstd[:, :], g.ps[0:96, 8:10], mybir.ActivationFunctionType.Sqrt,
                         bias=epsilon).then_inc(g.gn_s, 1)
def outlook_layer(nc, tag, images, x_in, x_out, w):
    f32 = mybir.dt.float32
    ALU, ACT, AX = mybir.AluOpType, mybir.ActivationFunctionType, mybir.AxisListType
    HEADS, TAPS, WINDOW = 6, 9, 25
    LOGITS = HEADS * TAPS * TAPS
    BLOCK = 2 * SIDE
    BLOCKS = PIX // BLOCK
    V_SIDE = SIDE + 4
    A_SIDE = SIDE + 2
    LINES = CHUNK // SIDE
    SCALE = 32 ** -0.5
    UNITS = CHUNKS * 2
    EVEN, ODD = (WINDOW + 1) // 2, WINDOW // 2

    with ExitStack() as ctx:
        def sb(name, shape, dt=f32):
            return ctx.enter_context(nc.sbuf_tensor(f"{tag}_{name}", shape, dt))

        def ps(name, shape):
            return ctx.enter_context(nc.psum_tensor(f"{tag}_{name}", shape, f32))

        def sem(name):
            return ctx.enter_context(nc.semaphore(f"{tag}_{name}"))

        g = Norm(sb, sem)
        x = g.x
        xn = sb("xn", [96, 2, PIX])
        v = sb("v", [96, 2, V_SIDE, V_SIDE])
        a = sb("a", [96, 6, A_SIDE * A_SIDE])
        prob = sb("prob", [BLOCK, 2, LOGITS])
        packed = sb("packed", [BLOCK, 2, 2, TAPS, 32])
        peak = sb("peak", [BLOCK, 2, HEADS * TAPS])
        total = sb("total", [BLOCK, 2, HEADS * TAPS])
        mix = sb("mix", [75, 2, CHUNK])
        prod = sb("prod", [96, 4, CHUNK])
        even = sb("even", [96, 2, CHUNK])
        odd = sb("odd", [96, 2, CHUNK])
        w_v = sb("w_v", [96, 2, 192])
        w_a = sb("w_a", [96, 2, LOGITS])
        b_a = sb("b_a", [1, LOGITS])
        w_p = sb("w_p", [96, 2, 192])
        b_p = sb("b_p", [96, 2])
        gather = sb("gather", [96, TAPS, 75])
        spread = sb("spread", [75, WINDOW, 96])
        ident = sb("ident", [BLOCK, BLOCK])
        one_row = sb("one_row", [1, BLOCK])
        eps = sb("eps", [96, 1])

        a_ps = [ps(f"a_ps{i}", [128, 512]) for i in range(2)]
        t_ps = [ps(f"t_ps{i}", [128, 512]) for i in range(2)]
        r_ps = [ps(f"r_ps{i}", [128, 512]) for i in range(3)]
        g.ps = ps("g_ps", [128, 512])

        (weights, consts, x_loaded, stored, v_done, v_copied, logit, peaked, shifted, exped, summed, inverted,
         packed_ok, turned, turned_out, mixed, mix_out, spread_ok, multiplied, add_even, add_odd, projected,
         added) = (
            sem(n) for n in
            "weights consts x_loaded stored v_done v_copied logit peaked shifted exped summed inverted "
            "packed_ok turned turned_out mixed mix_out spread_ok multiplied add_even add_odd projected "
            "added".split())

        a_grid = a.rearrange("p g (h w) -> p g h w", h=A_SIDE)
        block = ctx.enter_context(nc.Block())

        @block.sync
        def _(sp):
            for dst, name in ((w_v, "w_v"), (w_a, "w_a"), (b_a, "b_a"), (w_p, "w_p"), (b_p, "b_p"),
                              (gather, "gather"), (spread, "spread"), (g.group, "group"), (ident, "ident")):
                src = w[name]
                if name == "ident":
                    src = src[0:BLOCK, 0:BLOCK]
                sp.dma_start(dst[:], src).then_inc(weights, 16)
            with sp.Fori(0, images) as b:
                sp.wait_ge(stored, b * 16)
                sp.dma_start(x[:, :, :], x_in[b, :, :].rearrange("(k p) t -> p k t", k=2)).then_inc(x_loaded, 16)
                sp.wait_ge(added, b * CHUNKS + CHUNKS)
                sp.dma_start(x_out[b, :, :].rearrange("(k p) t -> p k t", k=2), x[:, :, :]).then_inc(stored, 16)
            sp.wait_ge(stored, images * 16)

        @block.gpsimd
        def _(pool):
            nc.gpsimd.memset(eps[:, :], 1e-5)
            nc.gpsimd.memset(one_row[:, :], 1.0)
            nc.gpsimd.memset(v[:, :, :, :], 0.0)
            nc.gpsimd.memset(a[:, :, :], 0.0)
            nc.gpsimd.memset(packed[:, :, :, :, :], 0.0).then_inc(consts, 1)
            pool.wait_ge(consts, 1)
            with pool.Fori(0, images) as b:
                for i in range(BLOCKS):
                    if i >= 2:
                        pool.wait_ge(turned, b * BLOCKS + i - 1)
                    pool.wait_ge(inverted, b * BLOCKS + i + 1)
                    for t in range(2):
                        source = prob[:, i % 2, t * 243:(t + 1) * 243].rearrange("p (n k q) -> p k n q", n=3, k=9)
                        scale = total[:, i % 2, t * 27:(t + 1) * 27].rearrange("p (n k) -> p k n", n=3)
                        for n in range(3):
                            last = nc.gpsimd.tensor_tensor(
                                packed[:, i % 2, t, :, n * 9:(n + 1) * 9], source[:, :, n, :],
                                scale[:, :, n:n + 1].to_broadcast([BLOCK, 9, 9]), ALU.mult)
                    last.then_inc(packed_ok, 1)
                for c in range(CHUNKS):
                    for t in range(2):
                        u = c * 2 + t
                        for e in range(1, EVEN):
                            d = 2 * e
                            k = u * (EVEN - 1) + e - 1
                            m = u * WINDOW + d
                            pool.wait_ge(multiplied, b * (UNITS * WINDOW) + m + 1)
                            if e >= 2:
                                pool.wait_ge(add_even, b * (UNITS * (EVEN - 1)) + k)
                            nc.gpsimd.tensor_tensor(even[:, t, :], even[:, t, :], prod[:, 2 * (k % 2), :],
                                                    ALU.add).then_inc(add_even, 1)

        @block.scalar
        def _(act):
            act.wait_ge(consts, 1)
            with act.Fori(0, images) as b:
                norm_scalar(nc, act, g, b, eps[0:96, :])
                for i in range(2 * CHUNKS):
                    t, c = divmod(i, CHUNKS)
                    act.wait_ge(v_done, b * (2 * CHUNKS) + i + 1)
                    nc.scalar.activation(v[:, t, 2 + c * LINES:2 + (c + 1) * LINES, 2:2 + SIDE],
                                         t_ps[i % 2][0:96, 0:CHUNK].rearrange("p (l s) -> p l s", l=LINES),
                                         ACT.Copy).then_inc(v_copied, 1)

                def turn_out(i):
                    act.wait_ge(turned, b * BLOCKS + i + 1)
                    for t in range(2):
                        last = nc.scalar.activation(
                            a_grid[:, 3 * t:3 * t + 3, 1 + 2 * i:3 + 2 * i, 1:1 + SIDE],
                            t_ps[t][0:96, 0:3 * BLOCK].rearrange("p (g l s) -> p g l s", g=3, l=2), ACT.Copy)
                    last.then_inc(turned_out, 1)
                for i in range(BLOCKS):
                    act.wait_ge(shifted, b * BLOCKS + i + 1)
                    nc.scalar.activation(prob[:, i % 2, :], prob[:, i % 2, :], ACT.Exp, scale=SCALE).then_inc(exped, 1)
                    if i >= 2:
                        turn_out(i - 2)
                turn_out(BLOCKS - 2)
                turn_out(BLOCKS - 1)
                for u in range(UNITS):
                    act.wait_ge(mixed, b * UNITS + u + 1)
                    nc.scalar.activation(mix[:, u % 2, :], t_ps[u % 2][0:75, 0:CHUNK], ACT.Copy).then_inc(mix_out, 1)

        @block.vector
        def _(dve):
            with dve.Fori(0, images) as b:
                norm_vector(nc, dve, g, b, xn, x_loaded)

                def finish(i):
                    dve.wait_ge(exped, b * BLOCKS + i + 1)
                    nc.vector.reduce_sum(total[:, i % 2, :], prob[:, i % 2, :].rearrange("p (r q) -> p r q", q=9),
                                         AX.X).then_inc(summed, 1)
                    dve.wait_ge(summed, b * BLOCKS + i + 1)
                    nc.vector.reciprocal(total[:, i % 2, :], total[:, i % 2, :]).then_inc(inverted, 1)
                for i in range(BLOCKS):
                    rows = a_ps[i % 2][0:BLOCK, 0:LOGITS].rearrange("p (r q) -> p r q", q=9)
                    dve.wait_ge(logit, b * BLOCKS + i + 1)
                    nc.vector.reduce_max(peak[:, i % 2, :], rows, AX.X).then_inc(peaked, 1)
                    if i >= 2:
                        dve.wait_ge(packed_ok, b * BLOCKS + i - 1)
                    dve.wait_ge(peaked, b * BLOCKS + i + 1)
                    nc.vector.tensor_tensor(prob[:, i % 2, :].rearrange("p (r q) -> p r q", q=9), rows,
                                            peak[:, i % 2, :].rearrange("p (r o) -> p r o", o=1)
                                            .to_broadcast([BLOCK, HEADS * TAPS, 9]), ALU.subtract).then_inc(shifted, 1)
                    if i >= 1:
                        finish(i - 1)
                finish(BLOCKS - 1)

                dve.wait_ge(v_copied, b * (2 * CHUNKS) + 2 * CHUNKS)
                for c in range(CHUNKS):
                    for t in range(2):
                        u = c * 2 + t
                        for d in range(WINDOW):
                            m = u * WINDOW + d
                            dy, dx = divmod(d, 5)
                            dve.wait_ge(spread_ok, b * (UNITS * WINDOW) + m + 1)
                            k = u * (EVEN - 1) + d // 2 - 1
                            if d < 2:
                                if c >= 1 and d == 0:
                                    dve.wait_ge(projected, b * CHUNKS + c)
                                dst = (even, odd)[d][:, t, :]
                            elif d % 2 == 0:
                                if k >= 2:
                                    dve.wait_ge(add_even, b * (UNITS * (EVEN - 1)) + k - 1)
                                dst = prod[:, 2 * (k % 2), :]
                            else:
                                dst = prod[:, 1 + 2 * ((d // 2) % 2), :]
                            nc.vector.tensor_tensor(
                                dst.rearrange("p (l s) -> p l s", l=LINES),
                                r_ps[m % 3][0:96, 0:CHUNK].rearrange("p (l s) -> p l s", l=LINES),
                                v[:, t, c * LINES + dy:(c + 1) * LINES + dy, dx:dx + SIDE],
                                ALU.mult).then_inc(multiplied, 1)
                            if d % 2 == 0 and d >= 4:
                                dve.wait_ge(multiplied, b * (UNITS * WINDOW) + m)
                                dve.wait_ge(add_odd, b * (UNITS * (ODD - 1)) + u * (ODD - 1) + d // 2 - 2)
                                nc.vector.tensor_tensor(odd[:, t, :], odd[:, t, :], prod[:, 1 + 2 * ((d // 2 - 1) % 2), :],
                                                        ALU.add).then_inc(add_odd, 1)
                    dve.wait_ge(projected, b * CHUNKS + c + 1)
                    for t in range(2):
                        cols = slice(c * CHUNK, (c + 1) * CHUNK)
                        last = nc.vector.scalar_tensor_tensor(x[:, t, cols], a_ps[t][0:96, 0:CHUNK], b_p[:, t:t + 1],
                                                              x[:, t, cols], ALU.add, ALU.add)
                    last.then_inc(added, 1)

        @block.tensor
        def _(pe):
            pe.wait_ge(weights, 9 * 16)
            pe.wait_ge(consts, 1)
            with pe.Fori(0, images) as b:
                norm_tensor(nc, pe, g, b)
                pe.wait_ge(g.gn_v, b * 8 + 8)
                for i in range(2 * CHUNKS):
                    t, c = divmod(i, CHUNKS)
                    if i >= 2:
                        pe.wait_ge(v_copied, b * (2 * CHUNKS) + i - 1)
                    for kt in range(2):
                        last = nc.tensor.matmul(t_ps[i % 2][0:96, 0:CHUNK], w_v[:, kt, t * 96:(t + 1) * 96],
                                                xn[:, kt, c * CHUNK:(c + 1) * CHUNK], start=kt == 0, stop=kt == 1)
                    last.then_inc(v_done, 1)

                def turn(i):
                    pe.wait_ge(packed_ok, b * BLOCKS + i + 1)
                    if i >= 1:
                        pe.wait_ge(turned_out, b * BLOCKS + i)
                    else:
                        pe.wait_ge(v_copied, b * (2 * CHUNKS) + 2 * CHUNKS)
                    for t in range(2):
                        for r in range(3):
                            last = nc.tensor.transpose(t_ps[t][0:96, r * BLOCK:(r + 1) * BLOCK],
                                                       packed[:, i % 2, t, 3 * r:3 * r + 3, :]
                                                       .rearrange("p k r -> p (k r)"), ident[:, :])
                    last.then_inc(turned, 1)
                for i in range(BLOCKS):
                    if i >= 2:
                        pe.wait_ge(shifted, b * BLOCKS + i - 1)
                    spot = slice(i * BLOCK, (i + 1) * BLOCK)
                    for kt in range(2):
                        nc.tensor.matmul(a_ps[i % 2][0:BLOCK, 0:LOGITS], xn[:, kt, spot], w_a[:, kt, :],
                                         start=kt == 0, stop=False)
                    nc.tensor.matmul(a_ps[i % 2][0:BLOCK, 0:LOGITS], one_row[:, :], b_a[:, :],
                                     start=False, stop=True).then_inc(logit, 1)
                    if i >= 2:
                        turn(i - 2)
                turn(BLOCKS - 2)
                turn(BLOCKS - 1)
                pe.wait_ge(turned_out, b * BLOCKS + BLOCKS)
                pe.wait_ge(shifted, b * BLOCKS + BLOCKS)

                def gathered(u):
                    c, t = divmod(u, 2)
                    if u >= 2:
                        pe.wait_ge(mix_out, b * UNITS + u - 1)
                    for k in range(TAPS):
                        i, j = divmod(k, 3)
                        last = nc.tensor.matmul(
                            t_ps[u % 2][0:75, 0:CHUNK], gather[:, k, :],
                            a_grid[:, 3 * t + k // 3, c * LINES + 2 - i:(c + 1) * LINES + 2 - i,
                                   2 - j:2 - j + SIDE], start=k == 0, stop=k == TAPS - 1)
                    last.then_inc(mixed, 1)
                gathered(0)
                for c in range(CHUNKS):
                    for t in range(2):
                        u = c * 2 + t
                        if u + 1 < UNITS:
                            gathered(u + 1)
                        pe.wait_ge(mix_out, b * UNITS + u + 1)
                        for d in range(WINDOW):
                            m = u * WINDOW + d
                            if m >= 3:
                                pe.wait_ge(multiplied, b * (UNITS * WINDOW) + m - 2)
                            nc.tensor.matmul(r_ps[m % 3][0:96, 0:CHUNK], spread[:, d, :], mix[:, u % 2, :],
                                             start=True, stop=True).then_inc(spread_ok, 1)
                    if c >= 1:
                        pe.wait_ge(added, b * CHUNKS + c)
                    pe.wait_ge(add_even, b * (UNITS * (EVEN - 1)) + (2 * c + 2) * (EVEN - 1))
                    pe.wait_ge(add_odd, b * (UNITS * (ODD - 1)) + (2 * c + 2) * (ODD - 1))
                    for m in range(2):
                        for t in range(2):
                            for s, source in enumerate((even, odd)):
                                last = nc.tensor.matmul(a_ps[m][0:96, 0:CHUNK], w_p[:, t, m * 96:(m + 1) * 96],
                                                        source[:, t, :], start=t + s == 0, stop=t + s == 2)
                    last.then_inc(projected, 1)
def ssm_layer(nc, tag, images, parts, tiles, double_bias, x_in, x_out, w):
    f32, bf16 = mybir.dt.float32, mybir.dt.bfloat16
    ALU, ACT = mybir.AluOpType, mybir.ActivationFunctionType
    P, NT = parts, tiles
    C = P * NT
    TASKS = 4 * NT
    UNITS = TASKS * CHUNKS
    STEPS = UNITS * STATES
    UNITS_DIR = NT * CHUNKS
    LINES = CHUNK // SIDE
    SLOTS = 4

    with ExitStack() as ctx:
        def sb(name, shape, dt=f32):
            return ctx.enter_context(nc.sbuf_tensor(f"{tag}_{name}", shape, dt))

        def ps(name, shape):
            return ctx.enter_context(nc.psum_tensor(f"{tag}_{name}", shape, f32))

        def sem(name):
            return ctx.enter_context(nc.semaphore(f"{tag}_{name}"))

        g = Norm(sb, sem)
        x = g.x
        xn_y = sb("xn_y", [128, NT, PIX])
        u = sb("u", [P, NT, PIX])
        pad_h = sb("pad_h", [128, max(STATES * CHUNK, 2 * PADDED)])
        bc = sb("bc", [128, PIX], bf16)
        dt_rs = sb("dt_rs", [128, PIX])
        delta = sb("delta", [P, 2, CHUNK])
        du = sb("du", [P, 2, CHUNK])
        sp_e = sb("sp_e", [P, CHUNK])
        sp_r = sb("sp_r", [P, CHUNK])
        sp_l = sb("sp_l", [P, CHUNK])
        sp_t = sb("sp_t", [P, CHUNK])
        decay_rest = sb("decay_rest", [128, 4, CHUNK])
        c_rep = sb("c_rep", [P, 4, CHUNK])
        hc = sb("hc", [P, 4, CHUNK])
        w_in = sb("w_in", [96, 2, 2 * C])
        w_xp = sb("w_xp", [P, NT, 4, 128])
        w_xd = sb("w_xd", [P, NT, 4, RANK])
        w_dt = sb("w_dt", [RANK, 4, C])
        w_out = sb("w_out", [P, NT, 192])
        dt_b = sb("dt_b", [P, 4, NT])
        a_neg = sb("a_neg", [P, 4 * NT, STATES])
        d_skip = sb("d_skip", [P, NT, 4])
        d_sum = sb("d_sum", [P, NT])
        conv_w = sb("conv_w", [P, NT, 9])
        conv_b = sb("conv_b", [P, NT])
        ln_g = sb("ln_g", [P, NT])
        ln_b = sb("ln_b", [P, NT])
        ones_c = sb("ones_c", [P, P])
        ident = sb("ident", [P, P])
        select = sb("select", [128, 2 * STATES, P], bf16)
        consts = sb("consts", [128, 3])

        b_ps = [ps(f"b_ps{i}", [128, 512]) for i in range(4)]
        c_ps = [ps(f"c_ps{i}", [128, 512]) for i in range(2)]
        y_ps = ps("y_ps", [128, 512])
        d_ps = ps("d_ps", [128, 512])
        g.ps = d_ps
        p_ps = b_ps[2:4]

        xn = xn_y[0:96, 0:2, :]
        y = xn_y[0:P, :, :]
        select_f32 = pad_h[:, 0:2 * STATES * P].rearrange("p (r c) -> p r c", r=2 * STATES)
        h = pad_h[0:P, 0:STATES * CHUNK].rearrange("p (n t) -> p n t", n=STATES)
        pads = [pad_h[0:P, i * PADDED:(i + 1) * PADDED].rearrange("p (a b) -> p a b", a=SIDE + 2)
                for i in range(2)]
        decay = decay_rest[0:P, :, :]
        rest = decay_rest[:, 0:2, :]
        square = decay[:, 0:NT, :]

        (weights, x_loaded, stored, ready, padded, inproj, inproj_out, conv, silu, skip,
         p1, hi, dtrow, split, dpre, log_s, series, log1p, delta_ok, du_ok, brep, crep, c_copied, mul_b, exped, scanned, hzero,
         hc_done, summed, y_out, e_mean, e_cent, e_sq, e_var, e_std, e_rstd,
         f_xn, f_z, f_silu, f_gate, f_out, f_add, relu_s, abs_s, exp_s, ln_s, clamped, squared) = (
            sem(n) for n in
            "weights x_loaded stored ready padded inproj inproj_out conv silu skip "
            "p1 hi dtrow split dpre log_s series log1p delta_ok du_ok brep crep c_copied mul_b exped scanned hzero "
            "hc_done summed y_out e_mean e_cent e_sq e_var e_std e_rstd "
            "f_xn f_z f_silu f_gate f_out f_add relu_s abs_s exp_s ln_s clamped squared".split())

        def grid(ap, order):
            return ap.rearrange("p (h w) -> p h w", h=SIDE) if order == 0 else \
                ap.rearrange("p (h w) -> p w h", h=SIDE)

        def part(buf, t, order, c):
            return grid(buf[:, t, :], order)[:, bass.ds(c * LINES, LINES), :]

        def lines(ap):
            return ap.rearrange("p (l s) -> p l s", l=LINES)

        def flip(ap, back):
            return ap[:, ::-1] if back else ap

        ORDER = [DIRS[tag][k][0] for k in range(4)]
        BACK = [DIRS[tag][k][1] for k in range(4)]

        def place(k, c):
            return c * -1 + (CHUNKS - 1) if BACK[k] else c

        def walk(engine, b, k, body):
            for t in range(NT):
                q0 = (k * NT + t) * CHUNKS
                with engine.Fori(0, CHUNKS // 2 - 1) as j:
                    for i in range(2):
                        body(t, j * 2 + i, q0 + i, j * 2, (t, j * 2 + i + 1))
                last = CHUNKS - 2
                body(t, last, q0 + last, 0, (t, last + 1))
                body(t, last + 1, q0 + last + 1, 0, (t + 1, 0) if t + 1 < NT else None)

        block = ctx.enter_context(nc.Block())

        @block.sync
        def _(sp):
            for dst, name in ((w_in, "w_in"), (w_xp, "w_xp"), (w_xd, "w_xd"), (w_dt, "w_dt"), (w_out, "w_out"),
                              (dt_b, "dt_b"), (a_neg, "a_log"), (d_skip, "d_skip"), (conv_w, "conv_w"),
                              (conv_b, "conv_b"), (ln_g, "ln_g"), (ln_b, "ln_b"), (g.group, "group"),
                              (ones_c, "ones_c"), (ident, "ident"), (select_f32, "select")):
                src = w[name]
                if name in ("ident",):
                    src = src[0:P, 0:P]
                if name == "select":
                    src = src[:, :, 0:P]
                sp.dma_start(dst[:], src).then_inc(weights, 16)
            with sp.Fori(0, images) as b:
                sp.wait_ge(stored, b * 16)
                sp.dma_start(x[:, :, :], x_in[b, :, :].rearrange("(k p) t -> p k t", k=2)).then_inc(x_loaded, 16)
                sp.wait_ge(f_add, b * CHUNKS + CHUNKS)
                sp.dma_start(x_out[b, :, :].rearrange("(k p) t -> p k t", k=2), x[:, :, :]).then_inc(stored, 16)
            sp.wait_ge(stored, images * 16)

        @block.gpsimd
        def _(pool):
            nc.gpsimd.memset(consts[:, 0:1], 1e-5)
            nc.gpsimd.memset(consts[:, 1:2], -math.log1p(SMALL))
            nc.gpsimd.memset(consts[:, 2:3], -0.75 * ROOT).then_inc(hc_done, SLOTS)
            with pool.Fori(0, images) as b:
                def prepare(k, t, c, q, qd, step):
                    pc = place(k, c)
                    if step == 0:
                        pool.wait_ge(log_s, b * UNITS + qd + q + 1)
                        pool.wait_ge(series, b * UNITS + qd + q + 1)
                        nc.gpsimd.tensor_tensor(sp_t[:, :], sp_l[:, :], sp_t[:, :], ALU.add).then_inc(log1p, 1)
                    if step == 1:
                        pool.wait_ge(log1p, b * UNITS + qd + q + 1)
                        if q >= 2 or not isinstance(qd, int):
                            pool.wait_ge(exped, b * STEPS + qd * STATES + max(0, (q - 1) * STATES))
                            pool.wait_ge(mul_b, b * STEPS + qd * STATES + max(0, (q - 1) * STATES))
                        nc.gpsimd.tensor_tensor(delta[:, q % 2, :], sp_r[:, :], sp_t[:, :], ALU.add).then_inc(delta_ok, 1)
                    if step == 2:
                        pool.wait_ge(delta_ok, b * UNITS + qd + q + 1)
                        nc.gpsimd.tensor_tensor(lines(du[:, q % 2, :]), lines(delta[:, q % 2, :]),
                                                part(u, t, ORDER[k], pc), ALU.mult).then_inc(du_ok, 1)

                for k in range(4):
                    for step in range(3):
                        prepare(k, 0, 0, k * UNITS_DIR, 0, step)

                    def chunk(t, c, q, qd, following):
                        for n in range(STATES):
                            s = q * STATES + n
                            if 8 <= n < 11 and following:
                                prepare(k, following[0], following[1], q + 1, qd, n - 8)
                            if s >= 4:
                                pool.wait_ge(summed, b * STEPS + qd * STATES + s - 3)
                            pool.wait_ge(c_copied, b * STEPS + qd * STATES + s + 1)
                            pool.wait_ge(scanned, b * STEPS + qd * STATES + s + 1)
                            nc.gpsimd.tensor_tensor(hc[:, n % 4, :], h[:, n, :], c_rep[:, n % 4, :],
                                                    ALU.mult).then_inc(hc_done, 1)
                    walk(pool, b, k, chunk)

        @block.scalar
        def _(act):
            act.wait_ge(weights, 16 * 16)
            nc.scalar.activation(select[:, :, :], select_f32, ACT.Copy).then_inc(ready, 1)
            nc.scalar.activation(a_neg[:, :, :], a_neg[:, :, :], ACT.Exp).then_inc(ready, 1)
            act.wait_ge(hc_done, SLOTS)
            with act.Fori(0, images) as b:
                norm_scalar(nc, act, g, b, consts[0:96, 0:1])
                act.wait_ge(padded, b + 1)
                for t in range(NT):
                    for c in range(CHUNKS):
                        i = t * CHUNKS + c
                        if c == 0 and t >= 2:
                            act.wait_ge(conv, b * (9 * NT) + 9 * (t - 1))
                        act.wait_ge(inproj, b * (NT * CHUNKS) + i + 1)
                        nc.scalar.activation(pads[t % 2][:, 1 + c * LINES:1 + (c + 1) * LINES, 1:1 + SIDE],
                                             lines(p_ps[i % 2][0:P, 0:CHUNK]), ACT.Copy).then_inc(inproj_out, 1)
                    if t >= 1:
                        act.wait_ge(conv, b * (9 * NT) + 9 * t)
                        nc.scalar.activation(u[:, t - 1, :], u[:, t - 1, :], ACT.Silu,
                                             bias=conv_b[:, t - 1:t]).then_inc(silu, 1)
                act.wait_ge(conv, b * (9 * NT) + 9 * NT)
                nc.scalar.activation(u[:, NT - 1, :], u[:, NT - 1, :], ACT.Silu,
                                     bias=conv_b[:, NT - 1:NT]).then_inc(silu, 1)

                def prepare(k, t, q, qd, step):
                    bias = dt_b[:, k, t:t + 1]
                    if step == 0:
                        act.wait_ge(dpre, b * UNITS + qd + q + 1)
                        act.wait_ge(delta_ok, b * UNITS + qd + q)
                        nc.scalar.activation(sp_e[:, :], d_ps[0:P, 0:CHUNK], ACT.Abs, bias=bias).then_inc(abs_s, 1)
                        nc.scalar.activation(sp_r[:, :], d_ps[0:P, 0:CHUNK], ACT.Relu, bias=bias).then_inc(relu_s, 1)
                    if step == 1:
                        act.wait_ge(abs_s, b * UNITS + qd + q + 1)
                        nc.scalar.activation(sp_e[:, :], sp_e[:, :], ACT.Exp, scale=-1.0).then_inc(exp_s, 1)
                    if step == 2:
                        act.wait_ge(exp_s, b * UNITS + qd + q + 1)
                        nc.scalar.activation(sp_l[:, :], sp_e[:, :], ACT.Ln, bias=1.0).then_inc(ln_s, 1)
                    if step == 3:
                        act.wait_ge(ln_s, b * UNITS + qd + q + 1)
                        nc.scalar.activation(sp_l[:, :], sp_l[:, :], ACT.Relu, bias=consts[0:P, 1:2]).then_inc(log_s, 1)

                def square_small(q, qd):
                    act.wait_ge(clamped, b * UNITS + qd + q + 1)
                    act.wait_ge(ln_s, b * UNITS + qd + q + 1)
                    nc.scalar.activation(sp_e[:, :], sp_t[:, :], ACT.Square, bias=consts[0:P, 2:3],
                                         scale=ROOT).then_inc(squared, 1)

                def exps(k, t, n, q, qd):
                    s = q * STATES + n
                    if n == 0:
                        act.wait_ge(delta_ok, b * UNITS + qd + q + 1)
                    if s >= 4:
                        act.wait_ge(scanned, b * STEPS + qd * STATES + s - 3)
                    nc.scalar.activation(decay[:, n % 4, :], delta[:, q % 2, :], ACT.Exp,
                                         scale=a_neg[:, k * NT + t, n:n + 1]).then_inc(exped, 1)

                def copy_c(n, q, qd):
                    s = q * STATES + n
                    act.wait_ge(crep, b * STEPS + qd * STATES + s + 1)
                    act.wait_ge(hc_done, b * STEPS + qd * STATES + s - 3 + SLOTS)
                    nc.scalar.activation(c_rep[:, n % 4, :], c_ps[n % 2][0:P, 0:CHUNK], ACT.Copy).then_inc(c_copied, 1)

                nc.scalar.preload_act_table_set("natural_log_exp_and_others")
                for k in range(4):
                    for c in range(CHUNKS):
                        n = k * CHUNKS + c
                        act.wait_ge(p1, b * (4 * CHUNKS) + n + 1)
                        nc.scalar.activation(bc[:, c * CHUNK:(c + 1) * CHUNK], p_ps[c % 2][:, 0:CHUNK],
                                             ACT.Copy).then_inc(hi, 1)
                        nc.scalar.activation(dt_rs[0:RANK, c * CHUNK:(c + 1) * CHUNK], c_ps[c % 2][0:RANK, 0:CHUNK],
                                             ACT.Copy).then_inc(dtrow, 1)
                    for step in range(4):
                        prepare(k, 0, k * UNITS_DIR, 0, step)
                    square_small(k * UNITS_DIR, 0)
                    for n in range(3):
                        exps(k, 0, n, k * UNITS_DIR, 0)
                    for n in range(2):
                        copy_c(n, k * UNITS_DIR, 0)

                    def chunk(t, c, q, qd, following):
                        for n in range(STATES):
                            if 1 <= n < 5 and following:
                                prepare(k, following[0], q + 1, qd, n - 1)
                            if n == 6 and following:
                                square_small(q + 1, qd)
                            if n + 2 < STATES:
                                copy_c(n + 2, q, qd)
                            elif following:
                                copy_c(n + 2 - STATES, q + 1, qd)
                            if n + 3 < STATES:
                                exps(k, t, n + 3, q, qd)
                            elif following:
                                exps(k, following[0], n + 3 - STATES, q + 1, qd)
                        act.wait_ge(summed, b * STEPS + qd * STATES + (q + 1) * STATES)
                        nc.scalar.activation(part(y, t, ORDER[k], place(k, c)), lines(y_ps[0:P, 0:CHUNK]),
                                             ACT.Copy).then_inc(y_out, 1)
                    walk(act, b, k, chunk)

                def std(c):
                    act.wait_ge(e_var, b * CHUNKS + c + 1)
                    nc.scalar.activation(dt_rs[0:P, c * CHUNK:(c + 1) * CHUNK], c_ps[c % 2][0:P, 0:CHUNK],
                                         ACT.Sqrt, bias=consts[0:P, 0:1]).then_inc(e_std, 1)
                for c in range(CHUNKS):
                    act.wait_ge(e_cent, b * CHUNKS + c + 1)
                    if c >= 1:
                        act.wait_ge(e_var, b * CHUNKS + c)
                    nc.scalar.activation(square[:, :, :], y[:, :, c * CHUNK:(c + 1) * CHUNK],
                                         ACT.Square).then_inc(e_sq, 1)
                    if c >= 1:
                        std(c - 1)
                std(CHUNKS - 1)
                for c in range(CHUNKS):
                    if c >= 1:
                        act.wait_ge(f_gate, b * (CHUNKS * 2 * NT) + c * 2 * NT)
                    for t in range(NT):
                        i = c * NT + t
                        act.wait_ge(f_z, b * (NT * CHUNKS) + i + 1)
                        nc.scalar.activation(square[:, t, :], p_ps[i % 2][0:P, 0:CHUNK], ACT.Silu).then_inc(f_silu, 1)

        @block.vector
        def _(dve):
            dve.wait_ge(ready, 2)
            dve.wait_ge(weights, 16 * 16)
            nc.vector.tensor_scalar(a_neg[:, :, :], a_neg[:, :, :], -1.0, None, ALU.mult).then_inc(ready, 1)
            nc.vector.reduce_sum(d_sum[:, :], d_skip[:, :, :], mybir.AxisListType.X).then_inc(ready, 1)
            if double_bias:
                nc.vector.tensor_scalar(dt_b[:, :, :], dt_b[:, :, :], 2.0, None, ALU.mult).then_inc(ready, 1)
            else:
                nc.vector.memset(g.stats[:, :, :, :], 0.0).then_inc(ready, 1)
            dve.wait_ge(ready, 5)
            with dve.Fori(0, images) as b:
                norm_vector(nc, dve, g, b, xn, x_loaded)
                dve.wait_ge(g.gn_v, b * 8 + 8)
                for i in range(2):
                    nc.vector.memset(pads[i][:, 0:SIDE + 2:SIDE + 1, :], 0.0)
                    last = nc.vector.memset(pads[i][:, 1:SIDE + 1, 0:SIDE + 2:SIDE + 1], 0.0)
                last.then_inc(padded, 1)
                for t in range(NT):
                    dve.wait_ge(inproj_out, b * (NT * CHUNKS) + (t + 1) * CHUNKS)
                    acc = grid(u[:, t, :], 0)
                    for tap in range(9):
                        shifted = pads[t % 2][:, tap // 3:tap // 3 + SIDE, tap % 3:tap % 3 + SIDE]
                        weight = conv_w[:, t, tap:tap + 1]
                        if tap == 0:
                            nc.vector.tensor_scalar(acc, shifted, weight, None, ALU.mult).then_inc(conv, 1)
                        else:
                            dve.wait_ge(conv, b * (9 * NT) + 9 * t + tap)
                            nc.vector.scalar_tensor_tensor(acc, shifted, weight, acc, ALU.mult,
                                                           ALU.add).then_inc(conv, 1)
                for t in range(NT):
                    dve.wait_ge(silu, b * NT + t + 1)
                    nc.vector.tensor_scalar(y[:, t, :], u[:, t, :], d_sum[:, t:t + 1], None, ALU.mult).then_inc(skip, 1)

                def mult(n, q, qd):
                    s = q * STATES + n
                    if n == 0:
                        dve.wait_ge(du_ok, b * UNITS + qd + q + 1)
                    dve.wait_ge(brep, b * STEPS + qd * STATES + s + 1)
                    bank = b_ps[n % 4][0:P, 0:CHUNK]
                    nc.vector.tensor_tensor(bank, du[:, q % 2, :], bank, ALU.mult).then_inc(mul_b, 1)

                def clamp(q, qd):
                    dve.wait_ge(exp_s, b * UNITS + qd + q + 1)
                    nc.vector.tensor_scalar(sp_t[:, :], sp_e[:, :], SMALL, None, ALU.min).then_inc(clamped, 1)

                def log_series(q, qd):
                    dve.wait_ge(squared, b * UNITS + qd + q + 1)
                    nc.vector.scalar_tensor_tensor(sp_t[:, :], sp_e[:, :], 13 / 16, sp_t[:, :], ALU.add,
                                                   ALU.mult).then_inc(series, 1)

                for k in range(4):
                    for c in range(CHUNKS):
                        n = k * CHUNKS + c
                        cols = slice(c * CHUNK, (c + 1) * CHUNK)
                        dve.wait_ge(hi, b * (4 * CHUNKS) + n + 1)
                        nc.vector.tensor_tensor(rest[64:128, c % 2, :], p_ps[c % 2][64:128, 0:CHUNK], bc[64:128, cols],
                                                ALU.subtract).then_inc(split, 1)
                        dve.wait_ge(split, b * (16 * CHUNKS) + 4 * n + 1)
                        nc.vector.tensor_copy(bc[64:128, cols], rest[64:128, c % 2, :]).then_inc(split, 1)
                        dve.wait_ge(split, b * (16 * CHUNKS) + 4 * n + 2)
                        nc.vector.tensor_tensor(rest[96:128, c % 2, :], rest[96:128, c % 2, :], bc[96:128, cols],
                                                ALU.subtract).then_inc(split, 1)
                        dve.wait_ge(split, b * (16 * CHUNKS) + 4 * n + 3)
                        nc.vector.tensor_copy(bc[96:128, cols], rest[96:128, c % 2, :]).then_inc(split, 1)
                    clamp(k * UNITS_DIR, 0)
                    log_series(k * UNITS_DIR, 0)
                    mult(0, k * UNITS_DIR, 0)
                    mult(1, k * UNITS_DIR, 0)
                    edge = slice(0, 1) if BACK[k] else slice(CHUNK - 1, CHUNK)

                    def clear(t):
                        task = k * NT + t
                        dve.wait_ge(hc_done, b * STEPS + task * (CHUNKS * STATES) + SLOTS)
                        nc.vector.memset(h[:, :, edge], 0.0).then_inc(hzero, 1)

                    def chunk(t, c, q, qd, following):
                        for n in range(STATES):
                            s = q * STATES + n
                            if n == 0:
                                dve.wait_ge(hzero, b * TASKS + k * NT + t + 1)
                            if n == 4:
                                dve.wait_ge(hc_done, b * STEPS + qd * STATES + q * STATES + SLOTS)
                            if n == 4 and following:
                                clamp(q + 1, qd)
                            if n == 7 and following:
                                log_series(q + 1, qd)
                            dve.wait_ge(mul_b, b * STEPS + qd * STATES + s + 1)
                            dve.wait_ge(exped, b * STEPS + qd * STATES + s + 1)
                            nc.vector.tensor_tensor_scan(flip(h[:, n, :], BACK[k]), flip(decay[:, n % 4, :], BACK[k]),
                                                         flip(b_ps[n % 4][0:P, 0:CHUNK], BACK[k]),
                                                         h[:, n, edge], ALU.mult, ALU.add).then_inc(scanned, 1)
                            if n + 2 < STATES:
                                mult(n + 2, q, qd)
                            elif following:
                                mult(n + 2 - STATES, q + 1, qd)
                        dve.wait_ge(hc_done, b * STEPS + qd * STATES + q * STATES + 4 + SLOTS)

                    for t in range(NT):
                        q0 = (k * NT + t) * CHUNKS
                        clear(t)
                        with dve.Fori(0, CHUNKS // 2 - 1) as j:
                            for i in range(2):
                                chunk(t, j * 2 + i, q0 + i, j * 2, (t, j * 2 + i + 1))
                        chunk(t, CHUNKS - 2, q0 + CHUNKS - 2, 0, (t, CHUNKS - 1))
                        chunk(t, CHUNKS - 1, q0 + CHUNKS - 1, 0, (t + 1, 0) if t + 1 < NT else None)

                def rstd(c):
                    dve.wait_ge(e_std, b * CHUNKS + c + 1)
                    cols = dt_rs[0:P, c * CHUNK:(c + 1) * CHUNK]
                    nc.vector.reciprocal(cols, cols).then_inc(e_rstd, 1)
                for c in range(CHUNKS):
                    dve.wait_ge(e_mean, b * CHUNKS + c + 1)
                    for t in range(NT):
                        cols = y[:, t, c * CHUNK:(c + 1) * CHUNK]
                        last = nc.vector.tensor_tensor(cols, cols, b_ps[c % 2][0:P, 0:CHUNK], ALU.subtract)
                    last.then_inc(e_cent, 1)
                    if c >= 1:
                        rstd(c - 1)
                rstd(CHUNKS - 1)

                def normed(c):
                    if c >= 1:
                        dve.wait_ge(f_z, b * (NT * CHUNKS) + c * NT)
                    for t in range(2):
                        last = nc.vector.tensor_scalar(hc[0:96, t, :], x[:, t, c * CHUNK:(c + 1) * CHUNK],
                                                       g.gmean[:, t:t + 1], g.grstd[:, t:t + 1], ALU.subtract, ALU.mult)
                    last.then_inc(f_xn, 1)
                normed(0)
                for c in range(CHUNKS):
                    cols = slice(c * CHUNK, (c + 1) * CHUNK)
                    dve.wait_ge(e_rstd, b * CHUNKS + c + 1)
                    for t in range(NT):
                        nc.vector.scalar_tensor_tensor(y[:, t, cols], y[:, t, cols], ln_g[:, t:t + 1],
                                                       dt_rs[0:P, cols], ALU.mult, ALU.mult).then_inc(f_gate, 1)
                    if c + 1 < CHUNKS:
                        normed(c + 1)
                    for t in range(NT):
                        dve.wait_ge(f_gate, b * (CHUNKS * 2 * NT) + c * 2 * NT + NT + t)
                        dve.wait_ge(f_silu, b * (NT * CHUNKS) + c * NT + t + 1)
                        nc.vector.scalar_tensor_tensor(y[:, t, cols], y[:, t, cols], ln_b[:, t:t + 1],
                                                       square[:, t, :], ALU.add, ALU.mult).then_inc(f_gate, 1)
                    dve.wait_ge(f_out, b * CHUNKS + c + 1)
                    for t in range(2):
                        last = nc.vector.tensor_tensor(x[:, t, cols], x[:, t, cols], b_ps[t][0:96, 0:CHUNK], ALU.add)
                    last.then_inc(f_add, 1)

        @block.tensor
        def _(pe):
            pe.wait_ge(weights, 16 * 16)
            pe.wait_ge(ready, 5)
            with pe.Fori(0, images) as b:
                norm_tensor(nc, pe, g, b)
                pe.wait_ge(g.gn_v, b * 8 + 8)
                for i in range(NT * CHUNKS):
                    t, c = divmod(i, CHUNKS)
                    if i >= 2:
                        pe.wait_ge(inproj_out, b * (NT * CHUNKS) + i - 1)
                    for kt in range(2):
                        last = nc.tensor.matmul(p_ps[i % 2][0:P, 0:CHUNK], w_in[:, kt, t * P:(t + 1) * P],
                                                xn[:, kt, c * CHUNK:(c + 1) * CHUNK], start=kt == 0, stop=kt == 1)
                    last.then_inc(inproj, 1)
                pe.wait_ge(inproj_out, b * (NT * CHUNKS) + NT * CHUNKS)
                pe.wait_ge(silu, b * NT + NT)

                def prepare(k, t, c, q, qd):
                    if q:
                        pe.wait_ge(log_s, b * UNITS + qd + q)
                    pc = place(k, c)
                    nc.tensor.matmul(d_ps[0:P, 0:CHUNK], w_dt[:, k, t * P:(t + 1) * P],
                                     dt_rs[0:RANK, bass.ds(pc * CHUNK, CHUNK)], start=True, stop=True).then_inc(dpre, 1)

                def broadcast(k, c, n, q, qd):
                    s = q * STATES + n
                    pc = place(k, c)
                    rows = bc[:, bass.ds(pc * CHUNK, CHUNK)]
                    if s >= 4:
                        pe.wait_ge(scanned, b * STEPS + qd * STATES + s - 3)
                    nc.tensor.matmul(b_ps[n % 4][0:P, 0:CHUNK], select[:, n, :], rows,
                                     start=True, stop=True).then_inc(brep, 1)
                    if s >= 2:
                        pe.wait_ge(c_copied, b * STEPS + qd * STATES + s - 1)
                    nc.tensor.matmul(c_ps[n % 2][0:P, 0:CHUNK], select[:, STATES + n, :], rows,
                                     start=True, stop=True).then_inc(crep, 1)

                for k in range(4):
                    if k:
                        pe.wait_ge(scanned, b * STEPS + k * UNITS_DIR * STATES)
                        pe.wait_ge(c_copied, b * STEPS + k * UNITS_DIR * STATES)
                    for c in range(CHUNKS):
                        n = k * CHUNKS + c
                        if c >= 2:
                            pe.wait_ge(split, b * (16 * CHUNKS) + 4 * (n - 2) + 1)
                            pe.wait_ge(dtrow, b * (4 * CHUNKS) + n - 1)
                        for t in range(NT):
                            nc.tensor.matmul(p_ps[c % 2][:, 0:CHUNK], w_xp[:, t, k, :], part(u, t, ORDER[k], c),
                                             start=t == 0, stop=t == NT - 1)
                        for t in range(NT):
                            last = nc.tensor.matmul(c_ps[c % 2][0:RANK, 0:CHUNK], w_xd[:, t, k, :],
                                                    part(u, t, ORDER[k], c), start=t == 0, stop=t == NT - 1)
                        last.then_inc(p1, 1)
                    pe.wait_ge(split, b * (16 * CHUNKS) + 4 * (k + 1) * CHUNKS)
                    pe.wait_ge(dtrow, b * (4 * CHUNKS) + (k + 1) * CHUNKS)
                    q0 = k * UNITS_DIR
                    prepare(k, 0, 0, q0, 0)
                    if k == 0:
                        pe.wait_ge(skip, b * NT + NT)
                    for n in range(3):
                        broadcast(k, 0, n, q0, 0)

                    def chunk(t, c, q, qd, following):
                        for n in range(STATES):
                            s = q * STATES + n
                            if n + 3 < STATES:
                                broadcast(k, c, n + 3, q, qd)
                            elif following:
                                broadcast(k, following[1], n + 3 - STATES, q + 1, qd)
                            if n == 0 and following:
                                prepare(k, following[0], following[1], q + 1, qd)
                            if n == 0:
                                pe.wait_ge(y_out, b * UNITS + qd + q)
                                nc.tensor.matmul(y_ps[0:P, 0:CHUNK], ident[:, :], part(y, t, ORDER[k], place(k, c)),
                                                 start=True, stop=False)
                            pe.wait_ge(hc_done, b * STEPS + qd * STATES + s + 1 + SLOTS)
                            nc.tensor.matmul(y_ps[0:P, 0:CHUNK], ident[:, :], hc[:, n % 4, :],
                                             start=False, stop=n == STATES - 1).then_inc(summed, 1)
                    walk(pe, b, k, chunk)

                pe.wait_ge(y_out, b * UNITS + UNITS)
                pe.wait_ge(scanned, b * STEPS + STEPS)

                def var(c):
                    pe.wait_ge(e_sq, b * CHUNKS + c + 1)
                    if c >= 2:
                        pe.wait_ge(e_std, b * CHUNKS + c - 1)
                    for t in range(NT):
                        last = nc.tensor.matmul(c_ps[c % 2][0:P, 0:CHUNK], ones_c[:, :], square[:, t, :],
                                                start=t == 0, stop=t == NT - 1)
                    last.then_inc(e_var, 1)
                for c in range(CHUNKS):
                    if c >= 2:
                        pe.wait_ge(e_cent, b * CHUNKS + c - 1)
                    for t in range(NT):
                        last = nc.tensor.matmul(b_ps[c % 2][0:P, 0:CHUNK], ones_c[:, :],
                                                y[:, t, c * CHUNK:(c + 1) * CHUNK], start=t == 0, stop=t == NT - 1)
                    last.then_inc(e_mean, 1)
                    if c >= 1:
                        var(c - 1)
                var(CHUNKS - 1)
                pe.wait_ge(e_cent, b * CHUNKS + CHUNKS)

                def gate(c):
                    pe.wait_ge(f_xn, b * CHUNKS + c + 1)
                    for t in range(NT):
                        i = c * NT + t
                        if i >= 2:
                            pe.wait_ge(f_silu, b * (NT * CHUNKS) + i - 1)
                        for kt in range(2):
                            last = nc.tensor.matmul(p_ps[i % 2][0:P, 0:CHUNK], w_in[:, kt, C + t * P:C + (t + 1) * P],
                                                    hc[0:96, kt, :], start=kt == 0, stop=kt == 1)
                        last.then_inc(f_z, 1)
                gate(0)
                for c in range(CHUNKS):
                    cols = slice(c * CHUNK, (c + 1) * CHUNK)
                    pe.wait_ge(f_gate, b * (CHUNKS * 2 * NT) + (c + 1) * 2 * NT)
                    if c >= 1:
                        pe.wait_ge(f_add, b * CHUNKS + c)
                    for m in range(2):
                        for t in range(NT):
                            last = nc.tensor.matmul(b_ps[m][0:96, 0:CHUNK], w_out[:, t, m * 96:(m + 1) * 96],
                                                    y[:, t, cols], start=t == 0, stop=t == NT - 1)
                    last.then_inc(f_out, 1)
                    if c + 1 < CHUNKS:
                        gate(c + 1)


def weight_tensors(nc, given):
    return {name: nc.dram_tensor(f"in_{name}", a.shape, mybir.dt.from_np(a.dtype), kind="ExternalInput").ap()
            for name, a in given.items()}
def recurrent_layer(nc, tag, images, x_in, x_out, w):
    f32 = mybir.dt.float32
    ALU, ACT = mybir.AluOpType, mybir.ActivationFunctionType
    SEQ = 2 * SIDE + 2

    with ExitStack() as ctx:
        def sb(name, shape, dt=f32):
            return ctx.enter_context(nc.sbuf_tensor(f"{tag}_{name}", shape, dt))

        def ps(name, shape):
            return ctx.enter_context(nc.psum_tensor(f"{tag}_{name}", shape, f32))

        def sem(name):
            return ctx.enter_context(nc.semaphore(f"{tag}_{name}"))

        g = Norm(sb, sem)
        x = g.x
        xn = sb("xn", [96, 2, PIX])
        bx = sb("bx", [96, 2, SIDE, SEQ])
        h = sb("h", [96, 2, SIDE, SEQ])
        acc = sb("acc", [96, 2, PIX])
        a_mat = sb("a_mat", [96, 2, 192])
        vecs = sb("vecs", [96, 4, 2])
        skip = sb("skip", [96, 2, 2])
        eps = sb("eps", [96, 1])
        h_ps = [ps(f"h_ps{m}", [128, 512]) for m in range(2)]
        g.ps = ps("g_ps", [128, 512])
        (weights, consts, ready, x_loaded, stored, bx_ok, moved, stepped, tail, tail_x) = (
            sem(n) for n in "weights consts ready x_loaded stored bx_ok moved stepped tail tail_x".split())
        MOVES = 2 * (SIDE - 1)
        STATES_OUT = 2 * SIDE

        def square(ap):
            return ap.rearrange("p (h w) -> p h w", h=SIDE)

        block = ctx.enter_context(nc.Block())

        @block.sync
        def _(sp):
            for dst, name in ((a_mat, "a_mat"), (vecs, "vecs"), (g.group, "group")):
                sp.dma_start(dst[:], w[name]).then_inc(weights, 16)
            with sp.Fori(0, images) as b:
                sp.wait_ge(stored, b * 16)
                sp.dma_start(x[:, :, :], x_in[b, :, :].rearrange("(k p) t -> p k t", k=2)).then_inc(x_loaded, 16)
                sp.wait_ge(tail_x, b * 8 + 8)
                sp.dma_start(x_out[b, :, :].rearrange("(k p) t -> p k t", k=2), x[:, :, :]).then_inc(stored, 16)
            sp.wait_ge(stored, images * 16)

        @block.gpsimd
        def _(pool):
            nc.gpsimd.memset(eps[:, :], 1e-5).then_inc(consts, 1)

        @block.scalar
        def _(act):
            act.wait_ge(consts, 1)
            with act.Fori(0, images) as b:
                norm_scalar(nc, act, g, b, eps[0:96, :])

        @block.vector
        def _(dve):
            dve.wait_ge(weights, 3 * 16)
            nc.vector.tensor_tensor(skip[:, 0, :], vecs[:, 2, :], vecs[:, 3, :], ALU.add).then_inc(ready, 1)
            dve.wait_ge(ready, 1)
            nc.vector.tensor_scalar(skip[:, 1, :], skip[:, 0, :], 2.0, None, ALU.mult).then_inc(ready, 1)
            dve.wait_ge(ready, 2)
            with dve.Fori(0, images) as b:
                norm_vector(nc, dve, g, b, xn, x_loaded)
                dve.wait_ge(g.gn_v, b * 8 + 8)
                for t in range(2):
                    bv = vecs[:, 0, t:t + 1]
                    nc.vector.tensor_scalar(bx[:, t, :, 0:SIDE], square(xn[:, t, :]), bv, None, ALU.mult)
                    nc.vector.tensor_scalar(bx[:, t, :, SIDE:2 * SIDE],
                                            square(xn[:, t, :]).rearrange("p h w -> p w h"), bv, None, ALU.mult)
                    nc.vector.tensor_scalar(bx[:, t, :, 2 * SIDE], xn[:, t, 0:PIX:SIDE + 1], bv, None, ALU.mult)
                    last = nc.vector.tensor_scalar(bx[:, t, :, 2 * SIDE + 1],
                                                   xn[:, t, SIDE - 1:PIX - 1:SIDE - 1], bv, None, ALU.mult)
                last.then_inc(bx_ok, 1)
                dve.wait_ge(bx_ok, b + 1)
                for m in range(2):
                    nc.vector.tensor_copy(h[:, m, 0, :], bx[:, m, 0, :]).then_inc(stepped, 1)
                with dve.Fori(1, SIDE) as s:
                    for m in range(2):
                        dve.wait_ge(moved, b * MOVES + s * 2 + (m - 1))
                        nc.vector.tensor_tensor(h[:, m, bass.ds(s, 1), :].rearrange("p a s -> p (a s)"),
                                                h_ps[m][0:96, 0:SEQ],
                                                bx[:, m, bass.ds(s, 1), :].rearrange("p a s -> p (a s)"),
                                                ALU.add).then_inc(stepped, 1)
                dve.wait_ge(stepped, b * STATES_OUT + STATES_OUT)
                for t in range(2):
                    nc.vector.tensor_tensor(square(acc[:, t, :]), h[:, t, :, 0:SIDE],
                                            h[:, t, :, SIDE:2 * SIDE].rearrange("p w h -> p h w"),
                                            ALU.add).then_inc(tail, 1)
                for t in range(2):
                    dve.wait_ge(tail, b * 6 + t + 1)
                    diag = acc[:, t, 0:PIX:SIDE + 1]
                    anti = acc[:, t, SIDE - 1:PIX - 1:SIDE - 1]
                    nc.vector.tensor_tensor(diag, diag, h[:, t, :, 2 * SIDE], ALU.add).then_inc(tail, 1)
                    nc.vector.tensor_tensor(anti, anti, h[:, t, :, 2 * SIDE + 1], ALU.add).then_inc(tail, 1)
                for t in range(2):
                    nc.vector.scalar_tensor_tensor(x[:, t, :], xn[:, t, :], skip[:, 1, t:t + 1], x[:, t, :],
                                                   ALU.mult, ALU.add).then_inc(tail_x, 1)
                dve.wait_ge(tail, b * 6 + 6)
                for t in range(2):
                    dve.wait_ge(tail_x, b * 8 + t + 1)
                    nc.vector.scalar_tensor_tensor(x[:, t, :], acc[:, t, :], vecs[:, 1, t:t + 1], x[:, t, :],
                                                   ALU.mult, ALU.add).then_inc(tail_x, 1)
                for t in range(2):
                    dve.wait_ge(tail_x, b * 8 + 3 + t)
                    for cells in (slice(0, PIX, SIDE + 1), slice(SIDE - 1, PIX - 1, SIDE - 1)):
                        nc.vector.scalar_tensor_tensor(x[:, t, cells], xn[:, t, cells], skip[:, 0, t:t + 1],
                                                       x[:, t, cells], ALU.mult, ALU.add).then_inc(tail_x, 1)

        @block.tensor
        def _(pe):
            pe.wait_ge(weights, 3 * 16)
            with pe.Fori(0, images) as b:
                norm_tensor(nc, pe, g, b)
                with pe.Fori(0, SIDE - 1) as s:
                    for kt in range(2):
                        state = h[:, kt, bass.ds(s, 1), :].rearrange("p a s -> p (a s)")
                        for m in range(2):
                            if kt == 0:
                                pe.wait_ge(stepped, b * STATES_OUT + s * 2 + (m + 1))
                            mm = nc.tensor.matmul(h_ps[m][0:96, 0:SEQ], a_mat[:, kt, m * 96:(m + 1) * 96], state,
                                                  start=kt == 0, stop=kt == 1)
                            if kt == 1:
                                mm.then_inc(moved, 1)
def _f(a):
    import numpy as np
    return np.ascontiguousarray(np.asarray(a))


def ssm_layout(parts, tiles, w_in, conv_w, conv_b, x_proj, dt_w, dt_b, a_log, d_skip, ln_g, ln_b, w_out):
    import numpy as np
    P, NT = parts, tiles

    def chans(a):
        return _f(np.moveaxis(a.reshape(NT, P, *a.shape[1:]), 0, 1))

    bc = x_proj[:, :, 12:44]
    xp = np.zeros((4, NT * P, 128), np.float32)
    for at in (0, 64, 96):
        xp[:, :, at:at + 32] = bc
    return {
        "w_in": _f(np.moveaxis(w_in.reshape(2, 96, -1), 0, 1)),
        "w_xp": chans(np.moveaxis(xp, 0, 1)),
        "w_xd": chans(np.moveaxis(x_proj[:, :, 0:12], 0, 1)),
        "w_dt": _f(np.moveaxis(dt_w, 0, 1)),
        "w_out": chans(w_out),
        "dt_b": _f(dt_b.reshape(4, NT, P).transpose(2, 0, 1)),
        "a_log": _f(a_log.reshape(4, NT, P, 16).transpose(2, 0, 1, 3).reshape(P, 4 * NT, 16)),
        "d_skip": _f(d_skip.reshape(4, NT, P).transpose(2, 1, 0)),
        "conv_w": chans(conv_w), "conv_b": chans(conv_b), "ln_g": chans(ln_g), "ln_b": chans(ln_b),
        "ones_c": np.full((P, P), 1.0 / (P * NT), np.float32),
    }


def constants():
    import numpy as np
    group = np.kron(np.eye(16), np.full((6, 6), 1 / 6)).astype(np.float32)
    select = np.zeros((128, 32, 128), np.float32)
    for n in range(32):
        for at in (0, 64, 96):
            select[at + n, n, :] = 1
    return {"group": group, "select": select, "ident": np.eye(128, dtype=np.float32)}


def outlook_layout(w_v, w_a, b_a, w_p, b_p):
    import numpy as np
    gather = np.zeros((96, 9, 75), np.float32)
    for k in range(9):
        for n in range(3):
            for q in range(9):
                dy, dx = q // 3 - k // 3 + 2, q % 3 - k % 3 + 2
                gather[32 * (k % 3) + 9 * n + q, k, 25 * n + 5 * dy + dx] = 1
    spread = np.zeros((75, 25, 96), np.float32)
    for n in range(3):
        for d in range(25):
            spread[25 * n + d, d, 32 * n:32 * n + 32] = 1

    def rows(a):
        return _f(np.moveaxis(a.reshape(2, 96, -1), 0, 1))
    return {"w_v": rows(w_v), "w_a": rows(w_a), "b_a": _f(b_a.reshape(1, -1)), "w_p": rows(w_p),
            "b_p": _f(b_p.reshape(2, 96).T), "gather": gather, "spread": spread}


def recurrent_layout(a_mat, bv, cv, dv, res_scale):
    import numpy as np
    vecs = [v.reshape(2, 96).T for v in (bv, cv, dv)] + [np.broadcast_to(res_scale, (96, 2))]
    return {"a_mat": _f(np.moveaxis(a_mat.reshape(2, 96, 192), 0, 1)), "vecs": _f(np.stack(vecs, 1))}


def _layers(a, layer):
    def get(name):
        return a[f"{layer}_conv_{name}"]
    if layer == "L0":
        g = outlook_layout(get("Wv"), get("Wa"), get("ba"), get("Wp"), get("bp"))
    elif layer == "L1":
        g = ssm_layout(96, 2, get("in_proj_w"), get("conv_w").reshape(192, 9), get("conv_b"), get("x_proj_w"),
                       get("dt_w"), get("dt_b"), get("A_logs"), get("Ds"), get("ln_g"), get("ln_b"), get("out_w"))
    elif layer == "L2":
        g = recurrent_layout(get("A"), get("Bv"), get("Cv"), get("Dv"), get("res_scale"))
    else:
        g = ssm_layout(128, 3, get("in_proj_w").T, get("conv_w").reshape(384, 9), get("conv_b"),
                       get("x_proj_weight").transpose(0, 2, 1), get("dt_projs_weight").transpose(0, 2, 1),
                       get("dt_projs_bias"), get("A_logs").reshape(4, 384, 16), get("Ds").reshape(4, 384),
                       get("norm_gamma"), get("norm_beta"), get("out_proj_w").T)
    return g


def kernel(**inputs):
    import numpy as np
    import concourse.bacc as _bacc
    from concourse.bass_utils import run_bass_kernel_spmd as _run
    a = {k: np.asarray(v) for k, v in inputs.items()}
    images = a["x"].shape[0]
    nc = _bacc.Bacc("TRN2", target_bir_lowering=False, num_devices=1)
    x = _f(a["x"].transpose(0, 3, 1, 2).reshape(images, 192, PIX))
    arrays = {"in_x": x}
    stream = nc.dram_tensor("in_x", x.shape, mybir.dt.float32, kind="ExternalInput").ap()
    shared = constants()
    arrays.update({f"in_{k}": v for k, v in shared.items()})
    shared = weight_tensors(nc, shared)
    for layer in LAYERS:
        given = _layers(a, layer)
        arrays.update({f"in_{layer}_{k}": v for k, v in given.items()})
        w = {**shared, **{k[len(layer) + 1:]: v for k, v in
                          weight_tensors(nc, {f"{layer}_{k}": v for k, v in given.items()}).items()}}
        last = layer == LAYERS[-1]
        out = nc.dram_tensor("out_x" if last else f"after_{layer}", x.shape, mybir.dt.float32,
                             kind="ExternalOutput" if last else "Internal").ap()
        if layer == "L0":
            outlook_layer(nc, layer, images, stream, out, w)
        elif layer == "L1":
            ssm_layer(nc, layer, images, 96, 2, True, stream, out, w)
        elif layer == "L2":
            recurrent_layer(nc, layer, images, stream, out, w)
        else:
            ssm_layer(nc, layer, images, 128, 3, False, stream, out, w)
        stream = out
    r = _run(nc, [arrays], core_ids=[0])
    return r.results[0]["out_x"].reshape(images, 192, SIDE, SIDE).transpose(0, 2, 3, 1)
```

```python
import math
import concourse.bass as bass
from concourse import mybir
from contextlib import ExitStack

SIDE = 56
PIX = SIDE * SIDE
CHUNK = 7 * SIDE
CHUNKS = PIX // CHUNK
PADDED = (SIDE + 2) * (SIDE + 2)
STATES = 16
RANK = 12
DIRS = {"L1": [(0, False), (0, True), (1, False), (1, True)],
        "L3": [(0, False), (1, False), (0, True), (1, True)]}
SMALL = 1 / 64
ROOT = math.sqrt(1 / 3)
LAYERS = ["L0", "L1", "L2", "L3"]
class Norm:

    def __init__(self, sb, sem):
        f32 = mybir.dt.float32
        self.x = sb("x", [96, 2, PIX], f32)
        self.stats = sb("stats", [96, 2, CHUNKS, 6], f32)
        self.mv = sb("mv", [96, 2, 2], f32)
        self.gmean = sb("gmean", [96, 2], f32)
        self.gdev = sb("gdev", [96, 2], f32)
        self.grstd = sb("grstd", [96, 2], f32)
        self.group = sb("group", [96, 96], f32)
        self.gn_v = sem("gn_v")
        self.gn_t = sem("gn_t")
        self.gn_s = sem("gn_s")


def norm_vector(nc, dve, g, b, xn, x_loaded, signals=16):
    ALU = mybir.AluOpType
    dve.wait_ge(x_loaded, b * signals + signals)
    for t in range(2):
        for c in range(CHUNKS):
            last = nc.vector.bn_stats(g.stats[:, t, c, :], g.x[:, t, c * CHUNK:(c + 1) * CHUNK])
    last.then_inc(g.gn_v, 1)
    dve.wait_ge(g.gn_v, b * 8 + 1)
    nc.vector.tensor_copy(g.gdev[:, :], g.stats[:, :, 0, 0])
    for t in range(2):
        last = nc.vector.bn_aggr(g.mv[:, t, :], g.stats[:, t, :, :])
    last.then_inc(g.gn_v, 1)
    dve.wait_ge(g.gn_t, b * 2 + 1)
    nc.vector.tensor_copy(g.gmean[:, :], g.ps[0:96, 0:2]).then_inc(g.gn_v, 1)
    dve.wait_ge(g.gn_v, b * 8 + 3)
    nc.vector.tensor_tensor(g.gdev[:, :], g.mv[:, :, 0], g.gmean[:, :], ALU.subtract).then_inc(g.gn_v, 1)
    dve.wait_ge(g.gn_v, b * 8 + 4)
    nc.vector.tensor_tensor(g.gdev[:, :], g.gdev[:, :], g.gdev[:, :], ALU.mult).then_inc(g.gn_v, 1)
    dve.wait_ge(g.gn_v, b * 8 + 5)
    nc.vector.tensor_tensor(g.gdev[:, :], g.gdev[:, :], g.mv[:, :, 1], ALU.add).then_inc(g.gn_v, 1)
    dve.wait_ge(g.gn_s, b + 1)
    nc.vector.reciprocal(g.grstd[:, :], g.grstd[:, :]).then_inc(g.gn_v, 1)
    dve.wait_ge(g.gn_v, b * 8 + 7)
    for t in range(2):
        last = nc.vector.tensor_scalar(xn[:, t, :], g.x[:, t, :], g.gmean[:, t:t + 1], g.grstd[:, t:t + 1],
                                       ALU.subtract, ALU.mult)
    last.then_inc(g.gn_v, 1)


def norm_tensor(nc, pe, g, b):
    pe.wait_ge(g.gn_v, b * 8 + 2)
    nc.tensor.matmul(g.ps[0:96, 0:2], g.group[:, :], g.mv[:, :, 0], start=True, stop=True).then_inc(g.gn_t, 1)
    pe.wait_ge(g.gn_v, b * 8 + 6)
    nc.tensor.matmul(g.ps[0:96, 8:10], g.group[:, :], g.gdev[:, :], start=True, stop=True).then_inc(g.gn_t, 1)


def norm_scalar(nc, act, g, b, epsilon):
    act.wait_ge(g.gn_t, b * 2 + 2)
    nc.scalar.activation(g.grstd[:, :], g.ps[0:96, 8:10], mybir.ActivationFunctionType.Sqrt,
                         bias=epsilon).then_inc(g.gn_s, 1)
def outlook_layer(nc, tag, images, x_in, x_out, w):
    f32 = mybir.dt.float32
    ALU, ACT, AX = mybir.AluOpType, mybir.ActivationFunctionType, mybir.AxisListType
    HEADS, TAPS, WINDOW = 6, 9, 25
    LOGITS = HEADS * TAPS * TAPS
    BLOCK = 2 * SIDE
    BLOCKS = PIX // BLOCK
    V_SIDE = SIDE + 4
    A_SIDE = SIDE + 2
    LINES = CHUNK // SIDE
    SCALE = 32 ** -0.5
    UNITS = CHUNKS * 2
    EVEN, ODD = (WINDOW + 1) // 2, WINDOW // 2

    with ExitStack() as ctx:
        def sb(name, shape, dt=f32):
            return ctx.enter_context(nc.sbuf_tensor(f"{tag}_{name}", shape, dt))

        def ps(name, shape):
            return ctx.enter_context(nc.psum_tensor(f"{tag}_{name}", shape, f32))

        def sem(name):
            return ctx.enter_context(nc.semaphore(f"{tag}_{name}"))

        g = Norm(sb, sem)
        x = g.x
        xn = sb("xn", [96, 2, PIX])
        v = sb("v", [96, 2, V_SIDE, V_SIDE])
        a = sb("a", [96, 6, A_SIDE * A_SIDE])
        prob = sb("prob", [BLOCK, 2, LOGITS])
        packed = sb("packed", [BLOCK, 2, 2, TAPS, 32])
        peak = sb("peak", [BLOCK, 2, HEADS * TAPS])
        total = sb("total", [BLOCK, 2, HEADS * TAPS])
        mix = sb("mix", [75, 2, CHUNK])
        prod = sb("prod", [96, 4, CHUNK])
        even = sb("even", [96, 2, CHUNK])
        odd = sb("odd", [96, 2, CHUNK])
        w_v = sb("w_v", [96, 2, 192])
        w_a = sb("w_a", [96, 2, LOGITS])
        b_a = sb("b_a", [1, LOGITS])
        w_p = sb("w_p", [96, 2, 192])
        b_p = sb("b_p", [96, 2])
        gather = sb("gather", [96, TAPS, 75])
        spread = sb("spread", [75, WINDOW, 96])
        ident = sb("ident", [BLOCK, BLOCK])
        one_row = sb("one_row", [1, BLOCK])
        eps = sb("eps", [96, 1])

        a_ps = [ps(f"a_ps{i}", [128, 512]) for i in range(2)]
        t_ps = [ps(f"t_ps{i}", [128, 512]) for i in range(2)]
        r_ps = [ps(f"r_ps{i}", [128, 512]) for i in range(3)]
        g.ps = ps("g_ps", [128, 512])

        (weights, consts, x_loaded, v_done, v_copied, logit, peaked, shifted, exped, summed, inverted,
         packed_ok, turned, turned_out, mixed, mix_out, spread_ok, multiplied, add_even, add_odd, projected,
         added) = (
            sem(n) for n in
            "weights consts x_loaded v_done v_copied logit peaked shifted exped summed inverted "
            "packed_ok turned turned_out mixed mix_out spread_ok multiplied add_even add_odd projected "
            "added".split())

        stored = [sem(f"stored{i}") for i in range(2)]
        a_grid = a.rearrange("p g (h w) -> p g h w", h=A_SIDE)
        block = ctx.enter_context(nc.Block())

        @block.sync
        def _(sp):
            for dst, name in ((w_v, "w_v"), (w_a, "w_a"), (b_a, "b_a"), (w_p, "w_p"), (b_p, "b_p"),
                              (gather, "gather"), (spread, "spread"), (g.group, "group"), (ident, "ident")):
                src = w[name]
                if name == "ident":
                    src = src[0:BLOCK, 0:BLOCK]
                sp.dma_start(dst[:], src).then_inc(weights, 16)

            def load(b, c):
                cols = slice(c * CHUNK, (c + 1) * CHUNK)
                sp.dma_start(x[:, :, cols], x_in[b, :, cols].rearrange("(k p) t -> p k t", k=2)).then_inc(x_loaded, 16)

            def store(b, c):
                cols = slice(c * CHUNK, (c + 1) * CHUNK)
                sp.wait_ge(added, b * CHUNKS + (c + 1))
                sp.dma_start(x_out[b, :, cols].rearrange("(k p) t -> p k t", k=2), x[:, :, cols]).then_inc(stored[c % 2], 16)

            for c in range(CHUNKS):
                load(0, c)
            if images > 1:
                with sp.Fori(0, images - 1) as b:
                    for c in range(CHUNKS + 1):
                        if c < CHUNKS:
                            store(b, c)
                        if c >= 1:
                            sp.wait_ge(stored[(c - 1) % 2], b * (8 * CHUNKS) + 16 * ((c - 1) // 2 + 1))
                            load(b + 1, c - 1)
            for c in range(CHUNKS):
                store(images - 1, c)
            for i in range(2):
                sp.wait_ge(stored[i], images * 8 * CHUNKS)

        @block.gpsimd
        def _(pool):
            nc.gpsimd.memset(eps[:, :], 1e-5)
            nc.gpsimd.memset(one_row[:, :], 1.0)
            nc.gpsimd.memset(v[:, :, :, :], 0.0)
            nc.gpsimd.memset(a[:, :, :], 0.0)
            nc.gpsimd.memset(packed[:, :, :, :, :], 0.0).then_inc(consts, 1)
            pool.wait_ge(consts, 1)
            with pool.Fori(0, images) as b:
                for i in range(BLOCKS):
                    if i >= 2:
                        pool.wait_ge(turned, b * BLOCKS + i - 1)
                    pool.wait_ge(inverted, b * BLOCKS + i + 1)
                    for t in range(2):
                        source = prob[:, i % 2, t * 243:(t + 1) * 243].rearrange("p (n k q) -> p k n q", n=3, k=9)
                        scale = total[:, i % 2, t * 27:(t + 1) * 27].rearrange("p (n k) -> p k n", n=3)
                        for n in range(3):
                            last = nc.gpsimd.tensor_tensor(
                                packed[:, i % 2, t, :, n * 9:(n + 1) * 9], source[:, :, n, :],
                                scale[:, :, n:n + 1].to_broadcast([BLOCK, 9, 9]), ALU.mult)
                    last.then_inc(packed_ok, 1)
                for c in range(CHUNKS):
                    for t in range(2):
                        u = c * 2 + t
                        for e in range(1, EVEN):
                            d = 2 * e
                            k = u * (EVEN - 1) + e - 1
                            m = u * WINDOW + d
                            pool.wait_ge(multiplied, b * (UNITS * WINDOW) + m + 1)
                            if e >= 2:
                                pool.wait_ge(add_even, b * (UNITS * (EVEN - 1)) + k)
                            nc.gpsimd.tensor_tensor(even[:, t, :], even[:, t, :], prod[:, 2 * (k % 2), :],
                                                    ALU.add).then_inc(add_even, 1)

        @block.scalar
        def _(act):
            act.wait_ge(consts, 1)
            with act.Fori(0, images) as b:
                norm_scalar(nc, act, g, b, eps[0:96, :])
                for i in range(2 * CHUNKS):
                    t, c = divmod(i, CHUNKS)
                    act.wait_ge(v_done, b * (2 * CHUNKS) + i + 1)
                    nc.scalar.activation(v[:, t, 2 + c * LINES:2 + (c + 1) * LINES, 2:2 + SIDE],
                                         t_ps[i % 2][0:96, 0:CHUNK].rearrange("p (l s) -> p l s", l=LINES),
                                         ACT.Copy).then_inc(v_copied, 1)

                def turn_out(i):
                    act.wait_ge(turned, b * BLOCKS + i + 1)
                    for t in range(2):
                        last = nc.scalar.activation(
                            a_grid[:, 3 * t:3 * t + 3, 1 + 2 * i:3 + 2 * i, 1:1 + SIDE],
                            t_ps[t][0:96, 0:3 * BLOCK].rearrange("p (g l s) -> p g l s", g=3, l=2), ACT.Copy)
                    last.then_inc(turned_out, 1)
                for i in range(BLOCKS):
                    act.wait_ge(shifted, b * BLOCKS + i + 1)
                    nc.scalar.activation(prob[:, i % 2, :], prob[:, i % 2, :], ACT.Exp, scale=SCALE).then_inc(exped, 1)
                    if i >= 2:
                        turn_out(i - 2)
                turn_out(BLOCKS - 2)
                turn_out(BLOCKS - 1)
                for u in range(UNITS):
                    act.wait_ge(mixed, b * UNITS + u + 1)
                    nc.scalar.activation(mix[:, u % 2, :], t_ps[u % 2][0:75, 0:CHUNK], ACT.Copy).then_inc(mix_out, 1)

        @block.vector
        def _(dve):
            with dve.Fori(0, images) as b:
                norm_vector(nc, dve, g, b, xn, x_loaded, 16 * CHUNKS)

                def finish(i):
                    dve.wait_ge(exped, b * BLOCKS + i + 1)
                    nc.vector.reduce_sum(total[:, i % 2, :], prob[:, i % 2, :].rearrange("p (r q) -> p r q", q=9),
                                         AX.X).then_inc(summed, 1)
                    dve.wait_ge(summed, b * BLOCKS + i + 1)
                    nc.vector.reciprocal(total[:, i % 2, :], total[:, i % 2, :]).then_inc(inverted, 1)
                for i in range(BLOCKS):
                    rows = a_ps[i % 2][0:BLOCK, 0:LOGITS].rearrange("p (r q) -> p r q", q=9)
                    dve.wait_ge(logit, b * BLOCKS + i + 1)
                    nc.vector.reduce_max(peak[:, i % 2, :], rows, AX.X).then_inc(peaked, 1)
                    if i >= 2:
                        dve.wait_ge(packed_ok, b * BLOCKS + i - 1)
                    dve.wait_ge(peaked, b * BLOCKS + i + 1)
                    nc.vector.tensor_tensor(prob[:, i % 2, :].rearrange("p (r q) -> p r q", q=9), rows,
                                            peak[:, i % 2, :].rearrange("p (r o) -> p r o", o=1)
                                            .to_broadcast([BLOCK, HEADS * TAPS, 9]), ALU.subtract).then_inc(shifted, 1)
                    if i >= 1:
                        finish(i - 1)
                finish(BLOCKS - 1)

                dve.wait_ge(v_copied, b * (2 * CHUNKS) + 2 * CHUNKS)
                for c in range(CHUNKS):
                    for t in range(2):
                        u = c * 2 + t
                        for d in range(WINDOW):
                            m = u * WINDOW + d
                            dy, dx = divmod(d, 5)
                            dve.wait_ge(spread_ok, b * (UNITS * WINDOW) + m + 1)
                            k = u * (EVEN - 1) + d // 2 - 1
                            if d < 2:
                                if c >= 1 and d == 0:
                                    dve.wait_ge(projected, b * CHUNKS + c)
                                dst = (even, odd)[d][:, t, :]
                            elif d % 2 == 0:
                                if k >= 2:
                                    dve.wait_ge(add_even, b * (UNITS * (EVEN - 1)) + k - 1)
                                dst = prod[:, 2 * (k % 2), :]
                            else:
                                dst = prod[:, 1 + 2 * ((d // 2) % 2), :]
                            nc.vector.tensor_tensor(
                                dst.rearrange("p (l s) -> p l s", l=LINES),
                                r_ps[m % 3][0:96, 0:CHUNK].rearrange("p (l s) -> p l s", l=LINES),
                                v[:, t, c * LINES + dy:(c + 1) * LINES + dy, dx:dx + SIDE],
                                ALU.mult).then_inc(multiplied, 1)
                            if d % 2 == 0 and d >= 4:
                                dve.wait_ge(multiplied, b * (UNITS * WINDOW) + m)
                                dve.wait_ge(add_odd, b * (UNITS * (ODD - 1)) + u * (ODD - 1) + d // 2 - 2)
                                nc.vector.tensor_tensor(odd[:, t, :], odd[:, t, :], prod[:, 1 + 2 * ((d // 2 - 1) % 2), :],
                                                        ALU.add).then_inc(add_odd, 1)
                    dve.wait_ge(projected, b * CHUNKS + c + 1)
                    for t in range(2):
                        cols = slice(c * CHUNK, (c + 1) * CHUNK)
                        last = nc.vector.scalar_tensor_tensor(x[:, t, cols], a_ps[t][0:96, 0:CHUNK], b_p[:, t:t + 1],
                                                              x[:, t, cols], ALU.add, ALU.add)
                    last.then_inc(added, 1)

        @block.tensor
        def _(pe):
            pe.wait_ge(weights, 9 * 16)
            pe.wait_ge(consts, 1)
            with pe.Fori(0, images) as b:
                norm_tensor(nc, pe, g, b)
                pe.wait_ge(g.gn_v, b * 8 + 8)
                for i in range(2 * CHUNKS):
                    t, c = divmod(i, CHUNKS)
                    if i >= 2:
                        pe.wait_ge(v_copied, b * (2 * CHUNKS) + i - 1)
                    for kt in range(2):
                        last = nc.tensor.matmul(t_ps[i % 2][0:96, 0:CHUNK], w_v[:, kt, t * 96:(t + 1) * 96],
                                                xn[:, kt, c * CHUNK:(c + 1) * CHUNK], start=kt == 0, stop=kt == 1)
                    last.then_inc(v_done, 1)

                def turn(i):
                    pe.wait_ge(packed_ok, b * BLOCKS + i + 1)
                    if i >= 1:
                        pe.wait_ge(turned_out, b * BLOCKS + i)
                    else:
                        pe.wait_ge(v_copied, b * (2 * CHUNKS) + 2 * CHUNKS)
                    for t in range(2):
                        for r in range(3):
                            last = nc.tensor.transpose(t_ps[t][0:96, r * BLOCK:(r + 1) * BLOCK],
                                                       packed[:, i % 2, t, 3 * r:3 * r + 3, :]
                                                       .rearrange("p k r -> p (k r)"), ident[:, :])
                    last.then_inc(turned, 1)
                for i in range(BLOCKS):
                    if i >= 2:
                        pe.wait_ge(shifted, b * BLOCKS + i - 1)
                    spot = slice(i * BLOCK, (i + 1) * BLOCK)
                    for kt in range(2):
                        nc.tensor.matmul(a_ps[i % 2][0:BLOCK, 0:LOGITS], xn[:, kt, spot], w_a[:, kt, :],
                                         start=kt == 0, stop=False)
                    nc.tensor.matmul(a_ps[i % 2][0:BLOCK, 0:LOGITS], one_row[:, :], b_a[:, :],
                                     start=False, stop=True).then_inc(logit, 1)
                    if i >= 2:
                        turn(i - 2)
                turn(BLOCKS - 2)
                turn(BLOCKS - 1)
                pe.wait_ge(turned_out, b * BLOCKS + BLOCKS)
                pe.wait_ge(shifted, b * BLOCKS + BLOCKS)

                def gathered(u):
                    c, t = divmod(u, 2)
                    if u >= 2:
                        pe.wait_ge(mix_out, b * UNITS + u - 1)
                    for k in range(TAPS):
                        i, j = divmod(k, 3)
                        last = nc.tensor.matmul(
                            t_ps[u % 2][0:75, 0:CHUNK], gather[:, k, :],
                            a_grid[:, 3 * t + k // 3, c * LINES + 2 - i:(c + 1) * LINES + 2 - i,
                                   2 - j:2 - j + SIDE], start=k == 0, stop=k == TAPS - 1)
                    last.then_inc(mixed, 1)
                gathered(0)
                for c in range(CHUNKS):
                    for t in range(2):
                        u = c * 2 + t
                        if u + 1 < UNITS:
                            gathered(u + 1)
                        pe.wait_ge(mix_out, b * UNITS + u + 1)
                        for d in range(WINDOW):
                            m = u * WINDOW + d
                            if m >= 3:
                                pe.wait_ge(multiplied, b * (UNITS * WINDOW) + m - 2)
                            nc.tensor.matmul(r_ps[m % 3][0:96, 0:CHUNK], spread[:, d, :], mix[:, u % 2, :],
                                             start=True, stop=True).then_inc(spread_ok, 1)
                    if c >= 1:
                        pe.wait_ge(added, b * CHUNKS + c)
                    pe.wait_ge(add_even, b * (UNITS * (EVEN - 1)) + (2 * c + 2) * (EVEN - 1))
                    pe.wait_ge(add_odd, b * (UNITS * (ODD - 1)) + (2 * c + 2) * (ODD - 1))
                    for m in range(2):
                        for t in range(2):
                            for s, source in enumerate((even, odd)):
                                last = nc.tensor.matmul(a_ps[m][0:96, 0:CHUNK], w_p[:, t, m * 96:(m + 1) * 96],
                                                        source[:, t, :], start=t + s == 0, stop=t + s == 2)
                    last.then_inc(projected, 1)
def ssm_layer(nc, tag, images, parts, tiles, double_bias, x_in, x_out, w):
    f32, bf16 = mybir.dt.float32, mybir.dt.bfloat16
    ALU, ACT = mybir.AluOpType, mybir.ActivationFunctionType
    P, NT = parts, tiles
    C = P * NT
    TASKS = 4 * NT
    UNITS = TASKS * CHUNKS
    STEPS = UNITS * STATES
    UNITS_DIR = NT * CHUNKS
    LINES = CHUNK // SIDE
    SLOTS = 4

    with ExitStack() as ctx:
        def sb(name, shape, dt=f32):
            return ctx.enter_context(nc.sbuf_tensor(f"{tag}_{name}", shape, dt))

        def ps(name, shape):
            return ctx.enter_context(nc.psum_tensor(f"{tag}_{name}", shape, f32))

        def sem(name):
            return ctx.enter_context(nc.semaphore(f"{tag}_{name}"))

        g = Norm(sb, sem)
        x = g.x
        xn_y = sb("xn_y", [128, NT, PIX])
        u = sb("u", [P, NT, PIX])
        pad_h = sb("pad_h", [128, max(STATES * CHUNK, 2 * PADDED)])
        bc = sb("bc", [128, PIX], bf16)
        dt_rs = sb("dt_rs", [128, PIX])
        delta = sb("delta", [P, 2, CHUNK])
        du = sb("du", [P, 2, CHUNK])
        sp_e = sb("sp_e", [P, CHUNK])
        sp_r = sb("sp_r", [P, CHUNK])
        sp_l = sb("sp_l", [P, CHUNK])
        sp_t = sb("sp_t", [P, CHUNK])
        decay_rest = sb("decay_rest", [128, 4, CHUNK])
        c_rep = sb("c_rep", [P, 4, CHUNK])
        hc = sb("hc", [P, 4, CHUNK])
        w_in = sb("w_in", [96, 2, 2 * C])
        w_xp = sb("w_xp", [P, NT, 4, 128])
        w_dt = sb("w_dt", [RANK, 4, C])
        w_out = sb("w_out", [P, NT, 192])
        dt_b = sb("dt_b", [P, 4, NT])
        a_neg = sb("a_neg", [P, 4 * NT, STATES])
        d_skip = sb("d_skip", [P, NT, 4])
        d_sum = sb("d_sum", [P, NT])
        conv_w = sb("conv_w", [P, NT, 9])
        conv_b = sb("conv_b", [P, NT])
        ln_g = sb("ln_g", [P, NT])
        ln_b = sb("ln_b", [P, NT])
        ones_c = sb("ones_c", [P, P])
        ident = sb("ident", [P, P])
        select = sb("select", [128, 2 * STATES, P], bf16)
        consts = sb("consts", [128, 4])

        b_ps = [ps(f"b_ps{i}", [128, 512]) for i in range(4)]
        c_ps = [ps(f"c_ps{i}", [128, 512]) for i in range(2)]
        yd_ps = [ps(f"yd_ps{i}", [128, 512]) for i in range(2)]
        g.ps = yd_ps[0]
        r_ps = b_ps[2:4] + c_ps
        p_ps = b_ps[2:4]

        dt_rows = dt_rs[0:RANK, :]
        xn = xn_y[0:96, 0:2, :]
        y = xn_y[0:P, :, :]
        select_f32 = pad_h[:, 0:2 * STATES * P].rearrange("p (r c) -> p r c", r=2 * STATES)
        h = pad_h[0:P, 0:STATES * CHUNK].rearrange("p (n t) -> p n t", n=STATES)
        pads = [pad_h[0:P, i * PADDED:(i + 1) * PADDED].rearrange("p (a b) -> p a b", a=SIDE + 2)
                for i in range(2)]
        decay = decay_rest[0:P, :, :]
        rest = decay_rest[:, :, :]
        gates = h[:, 0:2 * NT, :].rearrange("p (i t) c -> p i t c", i=2)
        square = decay[:, 0:NT, :]

        (weights, x_loaded, ready, padded, inproj, inproj_out, conv, silu, skip,
         p1, hi, dtrow, left, mid, left_low, low, dpre, log_s, series, log1p, delta_ok, du_ok, brep, crep, c_copied, mul_b, exped, scanned,
         hc_done, summed, y_out, e_mean, e_cent, e_sq, e_var, e_std, e_rstd,
         f_xn, f_z, f_silu, f_gate, f_out, f_add, relu_s, abs_s, exp_s, ln_s, clamped, squared) = (
            sem(n) for n in
            "weights x_loaded ready padded inproj inproj_out conv silu skip "
            "p1 hi dtrow left mid left_low low dpre log_s series log1p delta_ok du_ok brep crep c_copied mul_b exped scanned "
            "hc_done summed y_out e_mean e_cent e_sq e_var e_std e_rstd "
            "f_xn f_z f_silu f_gate f_out f_add relu_s abs_s exp_s ln_s clamped squared".split())

        stored = [sem(f"stored{i}") for i in range(2)]

        def grid(ap, order):
            return ap.rearrange("p (h w) -> p h w", h=SIDE) if order == 0 else \
                ap.rearrange("p (h w) -> p w h", h=SIDE)

        def part(buf, t, order, c):
            return grid(buf[:, t, :], order)[:, bass.ds(c * LINES, LINES), :]

        def lines(ap):
            return ap.rearrange("p (l s) -> p l s", l=LINES)

        def flip(ap, back):
            return ap[:, ::-1] if back else ap

        ORDER = [DIRS[tag][k][0] for k in range(4)]
        BACK = [DIRS[tag][k][1] for k in range(4)]

        def place(k, c):
            return c * -1 + (CHUNKS - 1) if BACK[k] else c

        def walk(engine, k, body):
            for t in range(NT):
                q0 = (k * NT + t) * CHUNKS
                body(t, 0, q0, 0, (t - 1, CHUNKS - 1) if t else None, (t, 1))
                with engine.Fori(0, (CHUNKS - 2) // 2) as j:
                    for i in range(2):
                        body(t, j * 2 + (i + 1), q0 + 1 + i, j * 2, (t, j * 2 + i), (t, j * 2 + (i + 2)))
                last = CHUNKS - 1
                body(t, last, q0 + last, 0, (t, last - 1), (t + 1, 0) if t + 1 < NT else None)

        block = ctx.enter_context(nc.Block())

        @block.sync
        def _(sp):
            for dst, name in ((w_in, "w_in"), (w_xp, "w_xp"), (w_dt, "w_dt"), (w_out, "w_out"),
                              (dt_b, "dt_b"), (a_neg, "a_log"), (d_skip, "d_skip"), (conv_w, "conv_w"),
                              (conv_b, "conv_b"), (ln_g, "ln_g"), (ln_b, "ln_b"), (g.group, "group"),
                              (ones_c, "ones_c"), (ident, "ident"), (select_f32, "select")):
                src = w[name]
                if name in ("ident",):
                    src = src[0:P, 0:P]
                if name == "select":
                    src = src[:, :, 0:P]
                sp.dma_start(dst[:], src).then_inc(weights, 16)

            def load(b, c):
                cols = slice(c * CHUNK, (c + 1) * CHUNK)
                sp.dma_start(x[:, :, cols], x_in[b, :, cols].rearrange("(k p) t -> p k t", k=2)).then_inc(x_loaded, 16)

            def store(b, c):
                cols = slice(c * CHUNK, (c + 1) * CHUNK)
                sp.wait_ge(f_add, b * CHUNKS + (c + 1))
                sp.dma_start(x_out[b, :, cols].rearrange("(k p) t -> p k t", k=2), x[:, :, cols]).then_inc(stored[c % 2], 16)

            for c in range(CHUNKS):
                load(0, c)
            if images > 1:
                with sp.Fori(0, images - 1) as b:
                    for c in range(CHUNKS + 1):
                        if c < CHUNKS:
                            store(b, c)
                        if c >= 1:
                            sp.wait_ge(stored[(c - 1) % 2], b * (8 * CHUNKS) + 16 * ((c - 1) // 2 + 1))
                            load(b + 1, c - 1)
            for c in range(CHUNKS):
                store(images - 1, c)
            for i in range(2):
                sp.wait_ge(stored[i], images * 8 * CHUNKS)

        @block.gpsimd
        def _(pool):
            nc.gpsimd.memset(consts[:, 0:1], 1e-5)
            nc.gpsimd.memset(consts[:, 1:2], -math.log1p(SMALL))
            nc.gpsimd.memset(consts[:, 3:4], 0.0)
            nc.gpsimd.memset(consts[:, 2:3], -0.75 * ROOT).then_inc(hc_done, SLOTS)
            with pool.Fori(0, images) as b:
                def log_sum(q, qd):
                    pool.wait_ge(log_s, b * UNITS + qd + q + 1)
                    pool.wait_ge(series, b * UNITS + qd + q + 1)
                    nc.gpsimd.tensor_tensor(sp_t[:, :], sp_l[:, :], sp_t[:, :], ALU.add).then_inc(log1p, 1)

                def times_u(k, t, c, q, qd):
                    pool.wait_ge(delta_ok, b * UNITS + qd + q + 1)
                    if q >= 2:
                        pool.wait_ge(mul_b, b * STEPS + qd * STATES + (q - 1) * STATES)
                    nc.gpsimd.tensor_tensor(lines(du[:, q % 2, :]), lines(delta[:, q % 2, :]),
                                            part(u, t, ORDER[k], place(k, c)), ALU.mult).then_inc(du_ok, 1)

                for k in range(4):
                    log_sum(k * UNITS_DIR, 0)
                    times_u(k, 0, 0, k * UNITS_DIR, 0)

                    def chunk(t, c, q, qd, before, following):
                        for n in range(STATES):
                            s = q * STATES + n
                            if n == 10 and following:
                                log_sum(q + 1, qd)
                            if n == 11 and following:
                                times_u(k, following[0], following[1], q + 1, qd)
                            if s >= 4:
                                pool.wait_ge(summed, b * STEPS + qd * STATES + s - 3)
                            pool.wait_ge(c_copied, b * STEPS + qd * STATES + s + 1)
                            pool.wait_ge(scanned, b * STEPS + qd * STATES + s + 1)
                            nc.gpsimd.tensor_tensor(hc[:, n % 4, :], h[:, n, :], c_rep[:, n % 4, :],
                                                    ALU.mult).then_inc(hc_done, 1)
                    walk(pool, k, chunk)

        @block.scalar
        def _(act):
            act.wait_ge(weights, 15 * 16)
            nc.scalar.activation(select[:, :, :], select_f32, ACT.Copy).then_inc(ready, 1)
            nc.scalar.activation(a_neg[:, :, :], a_neg[:, :, :], ACT.Exp).then_inc(ready, 1)
            act.wait_ge(hc_done, SLOTS)
            with act.Fori(0, images) as b:
                norm_scalar(nc, act, g, b, consts[0:96, 0:1])
                act.wait_ge(padded, b + 1)
                for t in range(NT):
                    for c in range(CHUNKS):
                        i = t * CHUNKS + c
                        if c == 0 and t >= 2:
                            act.wait_ge(conv, b * (9 * NT) + 9 * (t - 1))
                        act.wait_ge(inproj, b * (NT * CHUNKS) + i + 1)
                        nc.scalar.activation(pads[t % 2][:, 1 + c * LINES:1 + (c + 1) * LINES, 1:1 + SIDE],
                                             lines(p_ps[i % 2][0:P, 0:CHUNK]), ACT.Copy).then_inc(inproj_out, 1)
                    if t >= 1:
                        act.wait_ge(conv, b * (9 * NT) + 9 * t)
                        nc.scalar.activation(u[:, t - 1, :], u[:, t - 1, :], ACT.Silu,
                                             bias=conv_b[:, t - 1:t]).then_inc(silu, 1)
                act.wait_ge(conv, b * (9 * NT) + 9 * NT)
                nc.scalar.activation(u[:, NT - 1, :], u[:, NT - 1, :], ACT.Silu,
                                     bias=conv_b[:, NT - 1:NT]).then_inc(silu, 1)

                def prepare(k, t, q, qd, step):
                    bias = dt_b[:, k, t:t + 1]
                    if step == 0:
                        d_ps = yd_ps[q % 2]
                        act.wait_ge(dpre, b * UNITS + qd + q + 1)
                        act.wait_ge(delta_ok, b * UNITS + qd + q)
                        nc.scalar.activation(sp_e[:, :], d_ps[0:P, 0:CHUNK], ACT.Abs, bias=bias).then_inc(abs_s, 1)
                        nc.scalar.activation(sp_r[:, :], d_ps[0:P, 0:CHUNK], ACT.Relu, bias=bias).then_inc(relu_s, 1)
                    if step == 1:
                        act.wait_ge(abs_s, b * UNITS + qd + q + 1)
                        nc.scalar.activation(sp_e[:, :], sp_e[:, :], ACT.Exp, scale=-1.0).then_inc(exp_s, 1)
                    if step == 2:
                        act.wait_ge(exp_s, b * UNITS + qd + q + 1)
                        nc.scalar.activation(sp_l[:, :], sp_e[:, :], ACT.Ln, bias=1.0).then_inc(ln_s, 1)
                    if step == 3:
                        act.wait_ge(ln_s, b * UNITS + qd + q + 1)
                        nc.scalar.activation(sp_l[:, :], sp_l[:, :], ACT.Relu, bias=consts[0:P, 1:2]).then_inc(log_s, 1)

                def square_small(q, qd):
                    act.wait_ge(clamped, b * UNITS + qd + q + 1)
                    act.wait_ge(ln_s, b * UNITS + qd + q + 1)
                    nc.scalar.activation(sp_e[:, :], sp_t[:, :], ACT.Square, bias=consts[0:P, 2:3],
                                         scale=ROOT).then_inc(squared, 1)

                def exps(k, t, n, q, qd):
                    s = q * STATES + n
                    if n == 0:
                        act.wait_ge(delta_ok, b * UNITS + qd + q + 1)
                    if s >= 4:
                        act.wait_ge(scanned, b * STEPS + qd * STATES + s - 3)
                    nc.scalar.activation(decay[:, n % 4, :], delta[:, q % 2, :], ACT.Exp,
                                         scale=a_neg[:, k * NT + t, n:n + 1]).then_inc(exped, 1)

                def copy_c(n, q, qd):
                    s = q * STATES + n
                    act.wait_ge(crep, b * STEPS + qd * STATES + s + 1)
                    act.wait_ge(hc_done, b * STEPS + qd * STATES + s - 3 + SLOTS)
                    nc.scalar.activation(c_rep[:, n % 4, :], c_ps[n % 2][0:P, 0:CHUNK], ACT.Copy).then_inc(c_copied, 1)

                def flush(k, t, c, q, qd):
                    act.wait_ge(summed, b * STEPS + qd * STATES + (q + 1) * STATES)
                    nc.scalar.activation(part(y, t, ORDER[k], place(k, c)), lines(yd_ps[q % 2][0:P, 0:CHUNK]),
                                         ACT.Copy).then_inc(y_out, 1)

                nc.scalar.preload_act_table_set("natural_log_exp_and_others")
                for k in range(4):
                    for c in range(CHUNKS):
                        n = k * CHUNKS + c
                        act.wait_ge(p1, b * (4 * CHUNKS) + n + 1)
                        cols = slice(place(k, c) * CHUNK, (place(k, c) + 1) * CHUNK)
                        nc.scalar.activation(bc[:, cols], r_ps[c % 4][:, 0:CHUNK], ACT.Copy).then_inc(hi, 1)
                        nc.scalar.activation(dt_rows[:, cols], r_ps[c % 4][32:32 + RANK, 0:CHUNK],
                                             ACT.Copy).then_inc(dtrow, 1)
                        if 3 <= c < 7:
                            prepare(k, 0, k * UNITS_DIR, 0, c - 3)
                        if c == 6:
                            square_small(k * UNITS_DIR, 0)
                    for n in range(3):
                        exps(k, 0, n, k * UNITS_DIR, 0)
                    for n in range(2):
                        copy_c(n, k * UNITS_DIR, 0)

                    def chunk(t, c, q, qd, before, following):
                        for n in range(STATES):
                            if n == 2 and before:
                                flush(k, before[0], before[1], q - 1, qd)
                            if n in (4, 5, 6, 8) and following:
                                prepare(k, following[0], q + 1, qd, (4, 5, 6, 8).index(n))
                            if n == 7 and following:
                                square_small(q + 1, qd)
                            if n + 2 < STATES:
                                copy_c(n + 2, q, qd)
                            elif following:
                                copy_c(n + 2 - STATES, q + 1, qd)
                            if n + 3 < STATES:
                                exps(k, t, n + 3, q, qd)
                            elif following:
                                exps(k, following[0], n + 3 - STATES, q + 1, qd)
                        if not following:
                            flush(k, t, c, q, qd)
                    walk(act, k, chunk)

                def std(c):
                    act.wait_ge(e_var, b * CHUNKS + c + 1)
                    nc.scalar.activation(dt_rs[0:P, c * CHUNK:(c + 1) * CHUNK], c_ps[c % 2][0:P, 0:CHUNK],
                                         ACT.Sqrt, bias=consts[0:P, 0:1]).then_inc(e_std, 1)
                for c in range(CHUNKS):
                    act.wait_ge(e_cent, b * CHUNKS + c + 1)
                    if c >= 1:
                        act.wait_ge(e_var, b * CHUNKS + c)
                    nc.scalar.activation(square[:, :, :], y[:, :, c * CHUNK:(c + 1) * CHUNK],
                                         ACT.Square).then_inc(e_sq, 1)
                    if c >= 1:
                        std(c - 1)
                std(CHUNKS - 1)
                for c in range(CHUNKS):
                    if c >= 2:
                        act.wait_ge(f_gate, b * (CHUNKS * 2 * NT) + (c - 1) * 2 * NT)
                    for t in range(NT):
                        i = c * NT + t
                        act.wait_ge(f_z, b * (NT * CHUNKS) + i + 1)
                        nc.scalar.activation(gates[:, c % 2, t, :], p_ps[i % 2][0:P, 0:CHUNK], ACT.Silu).then_inc(f_silu, 1)

        @block.vector
        def _(dve):
            dve.wait_ge(ready, 2)
            dve.wait_ge(weights, 15 * 16)
            nc.vector.tensor_scalar(a_neg[:, :, :], a_neg[:, :, :], -1.0, None, ALU.mult).then_inc(ready, 1)
            nc.vector.reduce_sum(d_sum[:, :], d_skip[:, :, :], mybir.AxisListType.X).then_inc(ready, 1)
            if double_bias:
                nc.vector.tensor_scalar(dt_b[:, :, :], dt_b[:, :, :], 2.0, None, ALU.mult).then_inc(ready, 1)
            else:
                nc.vector.memset(g.stats[:, :, :, :], 0.0).then_inc(ready, 1)
            dve.wait_ge(ready, 5)
            with dve.Fori(0, images) as b:
                norm_vector(nc, dve, g, b, xn, x_loaded, 16 * CHUNKS)
                dve.wait_ge(g.gn_v, b * 8 + 8)
                for i in range(2):
                    nc.vector.memset(pads[i][:, 0:SIDE + 2:SIDE + 1, :], 0.0)
                    last = nc.vector.memset(pads[i][:, 1:SIDE + 1, 0:SIDE + 2:SIDE + 1], 0.0)
                last.then_inc(padded, 1)
                for t in range(NT):
                    dve.wait_ge(inproj_out, b * (NT * CHUNKS) + (t + 1) * CHUNKS)
                    acc = grid(u[:, t, :], 0)
                    for tap in range(9):
                        shifted = pads[t % 2][:, tap // 3:tap // 3 + SIDE, tap % 3:tap % 3 + SIDE]
                        weight = conv_w[:, t, tap:tap + 1]
                        if tap == 0:
                            nc.vector.tensor_scalar(acc, shifted, weight, None, ALU.mult).then_inc(conv, 1)
                        else:
                            dve.wait_ge(conv, b * (9 * NT) + 9 * t + tap)
                            nc.vector.scalar_tensor_tensor(acc, shifted, weight, acc, ALU.mult,
                                                           ALU.add).then_inc(conv, 1)
                for t in range(NT):
                    dve.wait_ge(silu, b * NT + t + 1)
                    nc.vector.tensor_scalar(y[:, t, :], u[:, t, :], d_sum[:, t:t + 1], None, ALU.mult).then_inc(skip, 1)

                def mult(n, q, qd):
                    s = q * STATES + n
                    if n == 0:
                        dve.wait_ge(du_ok, b * UNITS + qd + q + 1)
                    dve.wait_ge(brep, b * STEPS + qd * STATES + s + 1)
                    bank = b_ps[n % 4][0:P, 0:CHUNK]
                    nc.vector.tensor_tensor(bank, du[:, q % 2, :], bank, ALU.mult).then_inc(mul_b, 1)

                def clamp(q, qd):
                    dve.wait_ge(exp_s, b * UNITS + qd + q + 1)
                    nc.vector.tensor_scalar(sp_t[:, :], sp_e[:, :], SMALL, None, ALU.min).then_inc(clamped, 1)

                def log_series(q, qd):
                    dve.wait_ge(squared, b * UNITS + qd + q + 1)
                    nc.vector.scalar_tensor_tensor(sp_t[:, :], sp_e[:, :], 13 / 16, sp_t[:, :], ALU.add,
                                                   ALU.mult).then_inc(series, 1)

                def add_relu(q, qd):
                    dve.wait_ge(log1p, b * UNITS + qd + q + 1)
                    nc.vector.tensor_tensor(delta[:, q % 2, :], sp_r[:, :], sp_t[:, :], ALU.add).then_inc(delta_ok, 1)

                for k in range(4):
                    for c in range(CHUNKS + 1):
                        n = k * CHUNKS + c
                        if c == 6:
                            clamp(k * UNITS_DIR, 0)
                        if c == 8:
                            log_series(k * UNITS_DIR, 0)
                        cols, before = (slice(place(k, i) * CHUNK, (place(k, i) + 1) * CHUNK) for i in (c, c - 1))
                        if c < CHUNKS:
                            dve.wait_ge(hi, b * (4 * CHUNKS) + n + 1)
                            nc.vector.tensor_tensor(rest[64:128, c % 4, :], r_ps[c % 4][64:128, 0:CHUNK],
                                                    bc[64:128, cols], ALU.subtract).then_inc(left, 1)
                        if c >= 1:
                            dve.wait_ge(mid, b * (4 * CHUNKS) + n)
                            nc.vector.tensor_tensor(rest[96:128, (c - 1) % 4, :], rest[96:128, (c - 1) % 4, :],
                                                    bc[96:128, before], ALU.subtract).then_inc(left_low, 1)
                        if c < CHUNKS:
                            dve.wait_ge(left, b * (4 * CHUNKS) + n + 1)
                            nc.vector.tensor_copy(bc[64:128, cols], rest[64:128, c % 4, :]).then_inc(mid, 1)
                        if c >= 1:
                            dve.wait_ge(left_low, b * (4 * CHUNKS) + n)
                            nc.vector.tensor_copy(bc[96:128, before], rest[96:128, (c - 1) % 4, :]).then_inc(low, 1)
                    add_relu(k * UNITS_DIR, 0)
                    mult(0, k * UNITS_DIR, 0)
                    mult(1, k * UNITS_DIR, 0)
                    edge = slice(0, 1) if BACK[k] else slice(CHUNK - 1, CHUNK)

                    def chunk(t, c, q, qd, before, following):
                        for n in range(STATES):
                            s = q * STATES + n
                            if n == 0 and not before:
                                dve.wait_ge(hc_done, b * STEPS + q * STATES + SLOTS)
                            if n == 4:
                                dve.wait_ge(hc_done, b * STEPS + qd * STATES + q * STATES + SLOTS)
                            if n == 7 and following:
                                clamp(q + 1, qd)
                            if n == 11 and following:
                                add_relu(q + 1, qd)
                            dve.wait_ge(mul_b, b * STEPS + qd * STATES + s + 1)
                            dve.wait_ge(exped, b * STEPS + qd * STATES + s + 1)
                            nc.vector.tensor_tensor_scan(flip(h[:, n, :], BACK[k]), flip(decay[:, n % 4, :], BACK[k]),
                                                         flip(b_ps[n % 4][0:P, 0:CHUNK], BACK[k]),
                                                         consts[0:P, 3:4] if isinstance(c, int) and c == 0 else h[:, n, edge],
                                                         ALU.mult, ALU.add).then_inc(scanned, 1)
                            if n == 9 and following:
                                log_series(q + 1, qd)
                            if n + 2 < STATES:
                                mult(n + 2, q, qd)
                            elif following:
                                if n == STATES - 1:
                                    dve.wait_ge(hc_done, b * STEPS + qd * STATES + q * STATES + 4 + SLOTS)
                                mult(n + 2 - STATES, q + 1, qd)
                    walk(dve, k, chunk)

                def rstd(c):
                    dve.wait_ge(e_std, b * CHUNKS + c + 1)
                    cols = dt_rs[0:P, c * CHUNK:(c + 1) * CHUNK]
                    nc.vector.reciprocal(cols, cols).then_inc(e_rstd, 1)
                for c in range(CHUNKS):
                    dve.wait_ge(e_mean, b * CHUNKS + c + 1)
                    for t in range(NT):
                        cols = y[:, t, c * CHUNK:(c + 1) * CHUNK]
                        last = nc.vector.tensor_tensor(cols, cols, b_ps[c % 2][0:P, 0:CHUNK], ALU.subtract)
                    last.then_inc(e_cent, 1)
                    if c >= 2:
                        rstd(c - 2)
                rstd(CHUNKS - 2)
                rstd(CHUNKS - 1)

                def normed(c):
                    if c >= 2:
                        dve.wait_ge(f_z, b * (NT * CHUNKS) + (c - 1) * NT)
                    for t in range(2):
                        last = nc.vector.tensor_scalar(hc[0:96, c % 2 * 2 + t, :], x[:, t, c * CHUNK:(c + 1) * CHUNK],
                                                       g.gmean[:, t:t + 1], g.grstd[:, t:t + 1], ALU.subtract, ALU.mult)
                    last.then_inc(f_xn, 1)

                def residual(c):
                    dve.wait_ge(f_out, b * CHUNKS + c + 1)
                    for t in range(2):
                        cols = x[:, t, c * CHUNK:(c + 1) * CHUNK]
                        last = nc.vector.tensor_tensor(cols, cols, b_ps[t][0:96, 0:CHUNK], ALU.add)
                    last.then_inc(f_add, 1)

                normed(0)
                normed(1)
                for c in range(CHUNKS):
                    cols = slice(c * CHUNK, (c + 1) * CHUNK)
                    dve.wait_ge(e_rstd, b * CHUNKS + c + 1)
                    for t in range(NT):
                        nc.vector.scalar_tensor_tensor(y[:, t, cols], y[:, t, cols], ln_g[:, t:t + 1],
                                                       dt_rs[0:P, cols], ALU.mult, ALU.mult).then_inc(f_gate, 1)
                    for t in range(NT):
                        dve.wait_ge(f_gate, b * (CHUNKS * 2 * NT) + c * 2 * NT + t + 1)
                        dve.wait_ge(f_silu, b * (NT * CHUNKS) + c * NT + t + 1)
                        nc.vector.scalar_tensor_tensor(y[:, t, cols], y[:, t, cols], ln_b[:, t:t + 1],
                                                       gates[:, c % 2, t, :], ALU.add, ALU.mult).then_inc(f_gate, 1)
                    if c >= 1:
                        residual(c - 1)
                    if c + 2 < CHUNKS:
                        normed(c + 2)
                residual(CHUNKS - 1)

        @block.tensor
        def _(pe):
            pe.wait_ge(weights, 15 * 16)
            pe.wait_ge(ready, 5)
            with pe.Fori(0, images) as b:
                norm_tensor(nc, pe, g, b)
                pe.wait_ge(g.gn_v, b * 8 + 8)
                for i in range(NT * CHUNKS):
                    t, c = divmod(i, CHUNKS)
                    if i >= 2:
                        pe.wait_ge(inproj_out, b * (NT * CHUNKS) + i - 1)
                    for kt in range(2):
                        last = nc.tensor.matmul(p_ps[i % 2][0:P, 0:CHUNK], w_in[:, kt, t * P:(t + 1) * P],
                                                xn[:, kt, c * CHUNK:(c + 1) * CHUNK], start=kt == 0, stop=kt == 1)
                    last.then_inc(inproj, 1)
                pe.wait_ge(inproj_out, b * (NT * CHUNKS) + NT * CHUNKS)
                pe.wait_ge(silu, b * NT + NT)

                def prepare(k, t, c, q, qd):
                    if q >= 2:
                        pe.wait_ge(y_out, b * UNITS + qd + q - 1)
                    pc = place(k, c)
                    nc.tensor.matmul(yd_ps[q % 2][0:P, 0:CHUNK], w_dt[:, k, t * P:(t + 1) * P],
                                     dt_rows[:, bass.ds(pc * CHUNK, CHUNK)], start=True, stop=True).then_inc(dpre, 1)

                def broadcast_b(k, c, n, q, qd):
                    s = q * STATES + n
                    pc = place(k, c)
                    rows = bc[:, bass.ds(pc * CHUNK, CHUNK)]
                    if s >= 4:
                        pe.wait_ge(scanned, b * STEPS + qd * STATES + s - 3)
                    nc.tensor.matmul(b_ps[n % 4][0:P, 0:CHUNK], select[:, n, :], rows,
                                     start=True, stop=True).then_inc(brep, 1)

                def broadcast_c(k, c, n, q, qd):
                    s = q * STATES + n
                    pc = place(k, c)
                    rows = bc[:, bass.ds(pc * CHUNK, CHUNK)]
                    if s >= 2:
                        pe.wait_ge(c_copied, b * STEPS + qd * STATES + s - 1)
                    nc.tensor.matmul(c_ps[n % 2][0:P, 0:CHUNK], select[:, STATES + n, :], rows,
                                     start=True, stop=True).then_inc(crep, 1)

                def start_sum(k, t, c, q, qd):
                    pe.wait_ge(relu_s, b * UNITS + qd + q + 1)
                    nc.tensor.matmul(yd_ps[q % 2][0:P, 0:CHUNK], ident[:, :],
                                     part(y, t, ORDER[k], place(k, c)), start=True, stop=False)

                def add(n, q, qd):
                    s = q * STATES + n
                    pe.wait_ge(hc_done, b * STEPS + qd * STATES + s + 1 + SLOTS)
                    nc.tensor.matmul(yd_ps[q % 2][0:P, 0:CHUNK], ident[:, :], hc[:, n % 4, :],
                                     start=False, stop=n == STATES - 1).then_inc(summed, 1)

                for k in range(4):
                    if k:
                        pe.wait_ge(scanned, b * STEPS + k * UNITS_DIR * STATES)
                        pe.wait_ge(c_copied, b * STEPS + k * UNITS_DIR * STATES)
                    q0 = k * UNITS_DIR
                    for c in range(CHUNKS):
                        n = k * CHUNKS + c
                        if c >= 4:
                            pe.wait_ge(left, b * (4 * CHUNKS) + n - 3)
                            pe.wait_ge(dtrow, b * (4 * CHUNKS) + n - 3)
                        for t in range(NT):
                            last = nc.tensor.matmul(r_ps[c % 4][:, 0:CHUNK], w_xp[:, t, k, :], part(u, t, ORDER[k], place(k, c)),
                                                    start=t == 0, stop=t == NT - 1)
                        last.then_inc(p1, 1)
                        if c == 2:
                            pe.wait_ge(dtrow, b * (4 * CHUNKS) + k * CHUNKS + 1)
                            prepare(k, 0, 0, q0, 0)
                    pe.wait_ge(low, b * (4 * CHUNKS) + (k + 1) * CHUNKS)
                    pe.wait_ge(dtrow, b * (4 * CHUNKS) + (k + 1) * CHUNKS)
                    if k == 0:
                        pe.wait_ge(skip, b * NT + NT)
                    for n in range(4):
                        broadcast_b(k, 0, n, q0, 0)
                        broadcast_c(k, 0, n, q0, 0)
                    start_sum(k, 0, 0, q0, 0)

                    def chunk(t, c, q, qd, before, following):
                        for n in range(STATES):
                            s = q * STATES + n
                            ahead = (c, n + 4, q) if n + 4 < STATES else (following[1], n + 4 - STATES, q + 1) if following else None
                            if ahead:
                                broadcast_b(k, *ahead, qd)
                            if n == 2 and following:
                                prepare(k, following[0], following[1], q + 1, qd)
                            if n == 10 and following:
                                start_sum(k, following[0], following[1], q + 1, qd)
                            if n == 0:
                                if before:
                                    add(STATES - 1, q - 1, qd)
                            else:
                                add(n - 1, q, qd)
                            if ahead:
                                broadcast_c(k, *ahead, qd)
                        if not following:
                            add(STATES - 1, q, qd)
                    walk(pe, k, chunk)

                pe.wait_ge(y_out, b * UNITS + UNITS)
                pe.wait_ge(scanned, b * STEPS + STEPS)

                def var(c):
                    pe.wait_ge(e_sq, b * CHUNKS + c + 1)
                    if c >= 2:
                        pe.wait_ge(e_std, b * CHUNKS + c - 1)
                    for t in range(NT):
                        last = nc.tensor.matmul(c_ps[c % 2][0:P, 0:CHUNK], ones_c[:, :], square[:, t, :],
                                                start=t == 0, stop=t == NT - 1)
                    last.then_inc(e_var, 1)
                for c in range(CHUNKS):
                    if c >= 2:
                        pe.wait_ge(e_cent, b * CHUNKS + c - 1)
                    for t in range(NT):
                        last = nc.tensor.matmul(b_ps[c % 2][0:P, 0:CHUNK], ones_c[:, :],
                                                y[:, t, c * CHUNK:(c + 1) * CHUNK], start=t == 0, stop=t == NT - 1)
                    last.then_inc(e_mean, 1)
                    if c >= 1:
                        var(c - 1)
                var(CHUNKS - 1)
                pe.wait_ge(e_cent, b * CHUNKS + CHUNKS)

                def gate(c):
                    pe.wait_ge(f_xn, b * CHUNKS + c + 1)
                    for t in range(NT):
                        i = c * NT + t
                        if i >= 2:
                            pe.wait_ge(f_silu, b * (NT * CHUNKS) + i - 1)
                        for kt in range(2):
                            last = nc.tensor.matmul(p_ps[i % 2][0:P, 0:CHUNK], w_in[:, kt, C + t * P:C + (t + 1) * P],
                                                    hc[0:96, c % 2 * 2 + kt, :], start=kt == 0, stop=kt == 1)
                        last.then_inc(f_z, 1)
                gate(0)
                for c in range(CHUNKS):
                    cols = slice(c * CHUNK, (c + 1) * CHUNK)
                    if c + 1 < CHUNKS:
                        gate(c + 1)
                    pe.wait_ge(f_gate, b * (CHUNKS * 2 * NT) + (c + 1) * 2 * NT)
                    if c >= 1:
                        pe.wait_ge(f_add, b * CHUNKS + c)
                    for m in range(2):
                        for t in range(NT):
                            last = nc.tensor.matmul(b_ps[m][0:96, 0:CHUNK], w_out[:, t, m * 96:(m + 1) * 96],
                                                    y[:, t, cols], start=t == 0, stop=t == NT - 1)
                    last.then_inc(f_out, 1)


def weight_tensors(nc, given):
    return {name: nc.dram_tensor(f"in_{name}", a.shape, mybir.dt.from_np(a.dtype), kind="ExternalInput").ap()
            for name, a in given.items()}
def recurrent_layer(nc, tag, images, x_in, x_out, w):
    f32 = mybir.dt.float32
    ALU, ACT = mybir.AluOpType, mybir.ActivationFunctionType
    SEQ = 2 * SIDE + 2

    with ExitStack() as ctx:
        def sb(name, shape, dt=f32):
            return ctx.enter_context(nc.sbuf_tensor(f"{tag}_{name}", shape, dt))

        def ps(name, shape):
            return ctx.enter_context(nc.psum_tensor(f"{tag}_{name}", shape, f32))

        def sem(name):
            return ctx.enter_context(nc.semaphore(f"{tag}_{name}"))

        g = Norm(sb, sem)
        x = g.x
        xn = sb("xn", [96, 2, PIX])
        bx = sb("bx", [96, 2, SIDE, SEQ])
        h = sb("h", [96, 2, SIDE, SEQ])
        acc = sb("acc", [96, 2, PIX])
        a_mat = sb("a_mat", [96, 2, 192])
        vecs = sb("vecs", [96, 4, 2])
        skip = sb("skip", [96, 2, 2])
        eps = sb("eps", [96, 1])
        h_ps = [ps(f"h_ps{m}", [128, 512]) for m in range(2)]
        g.ps = ps("g_ps", [128, 512])
        (weights, consts, ready, x_loaded, stored, bx_ok, moved, stepped, tail, tail_x) = (
            sem(n) for n in "weights consts ready x_loaded stored bx_ok moved stepped tail tail_x".split())
        MOVES = 2 * (SIDE - 1)
        STATES_OUT = 2 * SIDE

        def square(ap):
            return ap.rearrange("p (h w) -> p h w", h=SIDE)

        block = ctx.enter_context(nc.Block())

        @block.sync
        def _(sp):
            for dst, name in ((a_mat, "a_mat"), (vecs, "vecs"), (g.group, "group")):
                sp.dma_start(dst[:], w[name]).then_inc(weights, 16)
            with sp.Fori(0, images) as b:
                sp.wait_ge(stored, b * 16)
                sp.dma_start(x[:, :, :], x_in[b, :, :].rearrange("(k p) t -> p k t", k=2)).then_inc(x_loaded, 16)
                sp.wait_ge(tail_x, b * 8 + 8)
                sp.dma_start(x_out[b, :, :].rearrange("(k p) t -> p k t", k=2), x[:, :, :]).then_inc(stored, 16)
            sp.wait_ge(stored, images * 16)

        @block.gpsimd
        def _(pool):
            nc.gpsimd.memset(eps[:, :], 1e-5).then_inc(consts, 1)

        @block.scalar
        def _(act):
            act.wait_ge(consts, 1)
            with act.Fori(0, images) as b:
                norm_scalar(nc, act, g, b, eps[0:96, :])

        @block.vector
        def _(dve):
            dve.wait_ge(weights, 3 * 16)
            nc.vector.tensor_tensor(skip[:, 0, :], vecs[:, 2, :], vecs[:, 3, :], ALU.add).then_inc(ready, 1)
            dve.wait_ge(ready, 1)
            nc.vector.tensor_scalar(skip[:, 1, :], skip[:, 0, :], 2.0, None, ALU.mult).then_inc(ready, 1)
            dve.wait_ge(ready, 2)
            with dve.Fori(0, images) as b:
                norm_vector(nc, dve, g, b, xn, x_loaded)
                dve.wait_ge(g.gn_v, b * 8 + 8)
                for t in range(2):
                    bv = vecs[:, 0, t:t + 1]
                    nc.vector.tensor_scalar(bx[:, t, :, 0:SIDE], square(xn[:, t, :]), bv, None, ALU.mult)
                    nc.vector.tensor_scalar(bx[:, t, :, SIDE:2 * SIDE],
                                            square(xn[:, t, :]).rearrange("p h w -> p w h"), bv, None, ALU.mult)
                    nc.vector.tensor_scalar(bx[:, t, :, 2 * SIDE], xn[:, t, 0:PIX:SIDE + 1], bv, None, ALU.mult)
                    last = nc.vector.tensor_scalar(bx[:, t, :, 2 * SIDE + 1],
                                                   xn[:, t, SIDE - 1:PIX - 1:SIDE - 1], bv, None, ALU.mult)
                last.then_inc(bx_ok, 1)
                dve.wait_ge(bx_ok, b + 1)
                for m in range(2):
                    nc.vector.tensor_copy(h[:, m, 0, :], bx[:, m, 0, :]).then_inc(stepped, 1)
                with dve.Fori(1, SIDE) as s:
                    for m in range(2):
                        dve.wait_ge(moved, b * MOVES + s * 2 + (m - 1))
                        nc.vector.tensor_tensor(h[:, m, bass.ds(s, 1), :].rearrange("p a s -> p (a s)"),
                                                h_ps[m][0:96, 0:SEQ],
                                                bx[:, m, bass.ds(s, 1), :].rearrange("p a s -> p (a s)"),
                                                ALU.add).then_inc(stepped, 1)
                dve.wait_ge(stepped, b * STATES_OUT + STATES_OUT)
                for t in range(2):
                    nc.vector.tensor_tensor(square(acc[:, t, :]), h[:, t, :, 0:SIDE],
                                            h[:, t, :, SIDE:2 * SIDE].rearrange("p w h -> p h w"),
                                            ALU.add).then_inc(tail, 1)
                for t in range(2):
                    dve.wait_ge(tail, b * 6 + t + 1)
                    diag = acc[:, t, 0:PIX:SIDE + 1]
                    anti = acc[:, t, SIDE - 1:PIX - 1:SIDE - 1]
                    nc.vector.tensor_tensor(diag, diag, h[:, t, :, 2 * SIDE], ALU.add).then_inc(tail, 1)
                    nc.vector.tensor_tensor(anti, anti, h[:, t, :, 2 * SIDE + 1], ALU.add).then_inc(tail, 1)
                for t in range(2):
                    nc.vector.scalar_tensor_tensor(x[:, t, :], xn[:, t, :], skip[:, 1, t:t + 1], x[:, t, :],
                                                   ALU.mult, ALU.add).then_inc(tail_x, 1)
                dve.wait_ge(tail, b * 6 + 6)
                for t in range(2):
                    dve.wait_ge(tail_x, b * 8 + t + 1)
                    nc.vector.scalar_tensor_tensor(x[:, t, :], acc[:, t, :], vecs[:, 1, t:t + 1], x[:, t, :],
                                                   ALU.mult, ALU.add).then_inc(tail_x, 1)
                for t in range(2):
                    dve.wait_ge(tail_x, b * 8 + 3 + t)
                    for cells in (slice(0, PIX, SIDE + 1), slice(SIDE - 1, PIX - 1, SIDE - 1)):
                        nc.vector.scalar_tensor_tensor(x[:, t, cells], xn[:, t, cells], skip[:, 0, t:t + 1],
                                                       x[:, t, cells], ALU.mult, ALU.add).then_inc(tail_x, 1)

        @block.tensor
        def _(pe):
            pe.wait_ge(weights, 3 * 16)
            with pe.Fori(0, images) as b:
                norm_tensor(nc, pe, g, b)
                with pe.Fori(0, SIDE - 1) as s:
                    for kt in range(2):
                        state = h[:, kt, bass.ds(s, 1), :].rearrange("p a s -> p (a s)")
                        for m in range(2):
                            if kt == 0:
                                pe.wait_ge(stepped, b * STATES_OUT + s * 2 + (m + 1))
                            mm = nc.tensor.matmul(h_ps[m][0:96, 0:SEQ], a_mat[:, kt, m * 96:(m + 1) * 96], state,
                                                  start=kt == 0, stop=kt == 1)
                            if kt == 1:
                                mm.then_inc(moved, 1)
def _f(a):
    import numpy as np
    return np.ascontiguousarray(np.asarray(a))


def ssm_layout(parts, tiles, w_in, conv_w, conv_b, x_proj, dt_w, dt_b, a_log, d_skip, ln_g, ln_b, w_out):
    import numpy as np
    P, NT = parts, tiles

    def chans(a):
        return _f(np.moveaxis(a.reshape(NT, P, *a.shape[1:]), 0, 1))

    bc = x_proj[:, :, 12:44]
    xp = np.zeros((4, NT * P, 128), np.float32)
    for at in (0, 64, 96):
        xp[:, :, at:at + 32] = bc
    xp[:, :, 32:44] = x_proj[:, :, 0:12]
    return {
        "w_in": _f(np.moveaxis(w_in.reshape(2, 96, -1), 0, 1)),
        "w_xp": chans(np.moveaxis(xp, 0, 1)),
        "w_dt": _f(np.moveaxis(dt_w, 0, 1)),
        "w_out": chans(w_out),
        "dt_b": _f(dt_b.reshape(4, NT, P).transpose(2, 0, 1)),
        "a_log": _f(a_log.reshape(4, NT, P, 16).transpose(2, 0, 1, 3).reshape(P, 4 * NT, 16)),
        "d_skip": _f(d_skip.reshape(4, NT, P).transpose(2, 1, 0)),
        "conv_w": chans(conv_w), "conv_b": chans(conv_b), "ln_g": chans(ln_g), "ln_b": chans(ln_b),
        "ones_c": np.full((P, P), 1.0 / (P * NT), np.float32),
    }


def constants():
    import numpy as np
    group = np.kron(np.eye(16), np.full((6, 6), 1 / 6)).astype(np.float32)
    select = np.zeros((128, 32, 128), np.float32)
    for n in range(32):
        for at in (0, 64, 96):
            select[at + n, n, :] = 1
    return {"group": group, "select": select, "ident": np.eye(128, dtype=np.float32)}


def outlook_layout(w_v, w_a, b_a, w_p, b_p):
    import numpy as np
    gather = np.zeros((96, 9, 75), np.float32)
    for k in range(9):
        for n in range(3):
            for q in range(9):
                dy, dx = q // 3 - k // 3 + 2, q % 3 - k % 3 + 2
                gather[32 * (k % 3) + 9 * n + q, k, 25 * n + 5 * dy + dx] = 1
    spread = np.zeros((75, 25, 96), np.float32)
    for n in range(3):
        for d in range(25):
            spread[25 * n + d, d, 32 * n:32 * n + 32] = 1

    def rows(a):
        return _f(np.moveaxis(a.reshape(2, 96, -1), 0, 1))
    return {"w_v": rows(w_v), "w_a": rows(w_a), "b_a": _f(b_a.reshape(1, -1)), "w_p": rows(w_p),
            "b_p": _f(b_p.reshape(2, 96).T), "gather": gather, "spread": spread}


def recurrent_layout(a_mat, bv, cv, dv, res_scale):
    import numpy as np
    vecs = [v.reshape(2, 96).T for v in (bv, cv, dv)] + [np.broadcast_to(res_scale, (96, 2))]
    return {"a_mat": _f(np.moveaxis(a_mat.reshape(2, 96, 192), 0, 1)), "vecs": _f(np.stack(vecs, 1))}


def _layers(a, layer):
    def get(name):
        return a[f"{layer}_conv_{name}"]
    if layer == "L0":
        g = outlook_layout(get("Wv"), get("Wa"), get("ba"), get("Wp"), get("bp"))
    elif layer == "L1":
        g = ssm_layout(96, 2, get("in_proj_w"), get("conv_w").reshape(192, 9), get("conv_b"), get("x_proj_w"),
                       get("dt_w"), get("dt_b"), get("A_logs"), get("Ds"), get("ln_g"), get("ln_b"), get("out_w"))
    elif layer == "L2":
        g = recurrent_layout(get("A"), get("Bv"), get("Cv"), get("Dv"), get("res_scale"))
    else:
        g = ssm_layout(128, 3, get("in_proj_w").T, get("conv_w").reshape(384, 9), get("conv_b"),
                       get("x_proj_weight").transpose(0, 2, 1), get("dt_projs_weight").transpose(0, 2, 1),
                       get("dt_projs_bias"), get("A_logs").reshape(4, 384, 16), get("Ds").reshape(4, 384),
                       get("norm_gamma"), get("norm_beta"), get("out_proj_w").T)
    return g


def kernel(**inputs):
    import numpy as np
    import concourse.bacc as _bacc
    from concourse.bass_utils import run_bass_kernel_spmd as _run
    a = {k: np.asarray(v) for k, v in inputs.items()}
    images = a["x"].shape[0]
    nc = _bacc.Bacc("TRN2", target_bir_lowering=False, num_devices=1)
    x = _f(a["x"].transpose(0, 3, 1, 2).reshape(images, 192, PIX))
    arrays = {"in_x": x}
    stream = nc.dram_tensor("in_x", x.shape, mybir.dt.float32, kind="ExternalInput").ap()
    shared = constants()
    arrays.update({f"in_{k}": v for k, v in shared.items()})
    shared = weight_tensors(nc, shared)
    for layer in LAYERS:
        given = _layers(a, layer)
        arrays.update({f"in_{layer}_{k}": v for k, v in given.items()})
        w = {**shared, **{k[len(layer) + 1:]: v for k, v in
                          weight_tensors(nc, {f"{layer}_{k}": v for k, v in given.items()}).items()}}
        last = layer == LAYERS[-1]
        out = nc.dram_tensor("out_x" if last else f"after_{layer}", x.shape, mybir.dt.float32,
                             kind="ExternalOutput" if last else "Internal").ap()
        if layer == "L0":
            outlook_layer(nc, layer, images, stream, out, w)
        elif layer == "L1":
            ssm_layer(nc, layer, images, 96, 2, True, stream, out, w)
        elif layer == "L2":
            recurrent_layer(nc, layer, images, stream, out, w)
        else:
            ssm_layer(nc, layer, images, 128, 3, False, stream, out, w)
        stream = out
    r = _run(nc, [arrays], core_ids=[0])
    return r.results[0]["out_x"].reshape(images, 192, SIDE, SIDE).transpose(0, 2, 3, 1)
```
